# Optimizing a Trainium2 kernel written in Bass

```python
import numpy as np
import jax
import jax.numpy as jnp

def _softmax(x, axis=-1):
    return jax.nn.softmax(x, axis=axis)

def _gelu(x):
    return jax.nn.gelu(x, approximate=True)

def _silu(x):
    return jax.nn.silu(x)

def _sigmoid(x):
    return jax.nn.sigmoid(x)

def _layernorm(x, axis=-1, eps=1e-05):
    m = jnp.mean(x, axis=axis, keepdims=True)
    v = jnp.var(x, axis=axis, keepdims=True)
    return (x - m) / jnp.sqrt(v + eps)

def _scatter_add(tgt, idx, src, axis=0):
    return tgt.at[idx].add(src)

def _segment_sum(src, seg, n):
    return jax.ops.segment_sum(src, seg, n)
kernel_name = 'mk_macaron_d1_jaxref_r8_61f9f3'

def setup_inputs(seed: int=0):
    np.random.seed(seed)
    _w = jnp.asarray

    def _L0_attn_setup():
        import jax, jax.numpy as jnp
        import numpy as np
        D_MODEL = 256
        D_STATE = 16
        D_CONV = 4
        EXPAND = 2
        D_INNER = EXPAND * D_MODEL
        HEAD_DIM = 64
        N_HEADS = D_INNER // HEAD_DIM
        N_GROUPS = 1
        CONV_DIM = D_INNER + 2 * N_GROUPS * D_STATE
        IN_DIM = D_INNER + CONV_DIM + N_HEADS
        BATCH, SEQ = (2, 512)
        EPS = 1e-05
        key = jax.random.key(seed)
        ks = jax.random.split(key, 8)
        s = 0.02
        return {'hidden_states': jax.random.normal(ks[0], (BATCH, SEQ, D_MODEL), jnp.float32), 'W_in': jax.random.normal(ks[1], (D_MODEL, IN_DIM), jnp.float32) * s, 'conv_w': jax.random.normal(ks[2], (CONV_DIM, D_CONV), jnp.float32) * s, 'conv_b': jnp.zeros((CONV_DIM,), jnp.float32), 'A_log': jnp.log(jax.random.uniform(ks[3], (N_HEADS,), jnp.float32, 1.0, 16.0)), 'D_skip': jnp.ones((N_HEADS,), jnp.float32), 'dt_bias': jnp.ones((N_HEADS,), jnp.float32), 'norm_w': jnp.ones((D_INNER,), jnp.float32), 'W_out': jax.random.normal(ks[4], (D_INNER, D_MODEL), jnp.float32) * s}
    _L0_attn_in = _L0_attn_setup()

    def _L0_ffn_setup():
        import jax, jax.numpy as jnp
        import numpy as np
        H = 256
        key = jax.random.key(seed)
        ks = jax.random.split(key, 10)
        s = 1.0 / np.sqrt(H)
        x = jax.random.normal(ks[0], (4, 256, H), dtype=jnp.float32)
        Wg = jax.random.uniform(ks[1], (2, H), jnp.float32, -s, s)
        W0a = jax.random.uniform(ks[2], (2 * H, H), jnp.float32, -s, s)
        b0a = jax.random.uniform(ks[3], (2 * H,), jnp.float32, -s, s)
        W0b = jax.random.uniform(ks[4], (H, 2 * H), jnp.float32, -s, s)
        b0b = jax.random.uniform(ks[5], (H,), jnp.float32, -s, s)
        W1a = jax.random.uniform(ks[6], (2 * H, H), jnp.float32, -s, s)
        b1a = jax.random.uniform(ks[7], (2 * H,), jnp.float32, -s, s)
        W1b = jax.random.uniform(ks[8], (H, 2 * H), jnp.float32, -s, s)
        b1b = jax.random.uniform(ks[9], (H,), jnp.float32, -s, s)
        return {'x': x, 'Wg': Wg, 'W0a': W0a, 'b0a': b0a, 'W0b': W0b, 'b0b': b0b, 'W1a': W1a, 'b1a': b1a, 'W1b': W1b, 'b1b': b1b}
    _L0_ffn_in = _L0_ffn_setup()
    _d = {'L0_attn_hidden_states': _L0_attn_in['hidden_states'], 'L0_attn_W_in': _L0_attn_in['W_in'], 'L0_attn_conv_w': _L0_attn_in['conv_w'], 'L0_attn_conv_b': _L0_attn_in['conv_b'], 'L0_attn_A_log': _L0_attn_in['A_log'], 'L0_attn_D_skip': _L0_attn_in['D_skip'], 'L0_attn_dt_bias': _L0_attn_in['dt_bias'], 'L0_attn_norm_w': _L0_attn_in['norm_w'], 'L0_attn_W_out': _L0_attn_in['W_out'], 'L0_ffn_Wg': _L0_ffn_in['Wg'], 'L0_ffn_W0a': _L0_ffn_in['W0a'], 'L0_ffn_b0a': _L0_ffn_in['b0a'], 'L0_ffn_W0b': _L0_ffn_in['W0b'], 'L0_ffn_b0b': _L0_ffn_in['b0b'], 'L0_ffn_W1a': _L0_ffn_in['W1a'], 'L0_ffn_b1a': _L0_ffn_in['b1a'], 'L0_ffn_W1b': _L0_ffn_in['W1b'], 'L0_ffn_b1b': _L0_ffn_in['b1b']}
    _x0 = _d['L0_attn_hidden_states']
    _d['L0_attn_hidden_states'] = jax.random.normal(jax.random.fold_in(jax.random.key(seed), 1), (16, 256, 256), dtype=_x0.dtype)
    del _x0
    return _d

def reference(L0_attn_hidden_states, L0_attn_W_in, L0_attn_conv_w, L0_attn_conv_b, L0_attn_A_log, L0_attn_D_skip, L0_attn_dt_bias, L0_attn_norm_w, L0_attn_W_out, L0_ffn_Wg, L0_ffn_W0a, L0_ffn_b0a, L0_ffn_W0b, L0_ffn_b0b, L0_ffn_W1a, L0_ffn_b1a, L0_ffn_W1b, L0_ffn_b1b):

    def _L0_attn_ref(hidden_states, W_in, conv_w, conv_b, A_log, D_skip, dt_bias, norm_w, W_out):
        import jax, jax.numpy as jnp
        import numpy as np
        D_MODEL = 256
        D_STATE = 16
        D_CONV = 4
        EXPAND = 2
        D_INNER = EXPAND * D_MODEL
        HEAD_DIM = 64
        N_HEADS = D_INNER // HEAD_DIM
        N_GROUPS = 1
        CONV_DIM = D_INNER + 2 * N_GROUPS * D_STATE
        IN_DIM = D_INNER + CONV_DIM + N_HEADS
        BATCH, SEQ = (2, 512)
        EPS = 1e-05
        b, l, _ = hidden_states.shape
        zxbcdt = jnp.einsum('bld,di->bli', hidden_states, W_in)
        gate = zxbcdt[..., :D_INNER]
        xBC = zxbcdt[..., D_INNER:D_INNER + CONV_DIM]
        dt = zxbcdt[..., D_INNER + CONV_DIM:]
        xpad = jnp.pad(xBC, ((0, 0), (D_CONV - 1, 0), (0, 0)))
        conv = conv_b
        for k in range(D_CONV):
            conv = conv + xpad[:, k:k + l, :] * conv_w[:, k]
        xBC = jax.nn.silu(conv)
        x = xBC[..., :D_INNER].reshape(b, l, N_HEADS, HEAD_DIM)
        Bm = xBC[..., D_INNER:D_INNER + D_STATE]
        Cm = xBC[..., D_INNER + D_STATE:]
        dt = jax.nn.softplus(dt + dt_bias)
        A = -jnp.exp(A_log)
        dA = jnp.exp(dt * A)
        xs = x.transpose(1, 0, 2, 3)
        Bs = Bm.transpose(1, 0, 2)
        Cs = Cm.transpose(1, 0, 2)
        dts = dt.transpose(1, 0, 2)
        dAs = dA.transpose(1, 0, 2)
        h0 = jnp.zeros((b, N_HEADS, HEAD_DIM, D_STATE), hidden_states.dtype)

        def step(h, inp):
            x_t, B_t, C_t, dt_t, dA_t = inp
            h = h * dA_t[:, :, None, None] + (dt_t[:, :, None] * x_t)[..., None] * B_t[:, None, None, :]
            y = jnp.einsum('bhpn,bn->bhp', h, C_t)
            return (h, y)
        _, ys = jax.lax.scan(step, h0, (xs, Bs, Cs, dts, dAs))
        y = ys.transpose(1, 0, 2, 3) + D_skip[None, None, :, None] * x
        y = y.reshape(b, l, D_INNER)
        y = y * jax.nn.silu(gate)
        var = jnp.mean(y * y, axis=-1, keepdims=True)
        y = y * jax.lax.rsqrt(var + EPS) * norm_w
        return jnp.einsum('bld,do->blo', y, W_out)

    def _L0_ffn_ref(x, Wg, W0a, b0a, W0b, b0b, W1a, b1a, W1b, b1b):
        import jax, jax.numpy as jnp
        import numpy as np
        H = 256
        scores = jax.nn.softmax(jnp.einsum('bsh,eh->bse', x, Wg), axis=-1)
        top_expert = jnp.argmax(scores, axis=-1)
        h0 = jax.nn.gelu(jnp.einsum('bsh,fh->bsf', x, W0a) + b0a, approximate=False)
        out0 = jnp.einsum('bsf,hf->bsh', h0, W0b) + b0b
        h1 = jax.nn.relu(jnp.einsum('bsh,fh->bsf', x, W1a) + b1a)
        out1 = jnp.einsum('bsf,hf->bsh', h1, W1b) + b1b
        mask0 = (top_expert == 0).astype(x.dtype)[..., None]
        return out0 * mask0 + out1 * (1.0 - mask0)
    x = L0_attn_hidden_states
    x = x + 0.5 * _L0_ffn_ref(_layernorm(x, axis=-1), L0_ffn_Wg, L0_ffn_W0a, L0_ffn_b0a, L0_ffn_W0b, L0_ffn_b0b, L0_ffn_W1a, L0_ffn_b1a, L0_ffn_W1b, L0_ffn_b1b)
    x = x + _L0_attn_ref(_layernorm(x, axis=-1), L0_attn_W_in, L0_attn_conv_w, L0_attn_conv_b, L0_attn_A_log, L0_attn_D_skip, L0_attn_dt_bias, L0_attn_norm_w, L0_attn_W_out)
    x = x + 0.5 * _L0_ffn_ref(_layernorm(x, axis=-1), L0_ffn_Wg, L0_ffn_W0a, L0_ffn_b0a, L0_ffn_W0b, L0_ffn_b0b, L0_ffn_W1a, L0_ffn_b1a, L0_ffn_W1b, L0_ffn_b1b)
    return x

_drawn_inputs = setup_inputs


def setup_inputs(seed=0):
    import zlib

    import numpy as np

    out = dict(_drawn_inputs(seed))
    spreads = {'L0_attn_conv_b': (0.0, 0.1),
     'L0_attn_D_skip': (1.0, 0.2),
     'L0_attn_dt_bias': (1.0, 0.6),
     'L0_attn_norm_w': (1.0, 0.2)}
    factors = {'L0_attn_A_log': 64.0, 'L0_ffn_b0a': 4.591, 'L0_ffn_b1a': 3.376}
    for name, (base, spread) in spreads.items():
        noise = np.random.default_rng([zlib.crc32(name.encode()), seed]).standard_normal(out[name].shape)
        drawn = base * np.exp(spread * noise) if base else spread * noise
        out[name] = jnp.asarray(drawn.astype(out[name].dtype))
    for name, factor in factors.items():
        out[name] = (out[name] * factor).astype(out[name].dtype)
    return out
```

```python
from contextlib import ExitStack

import concourse.bass as bass
from concourse import mybir

F32 = mybir.dt.float32
F32R = mybir.dt.float32r
ALU = mybir.AluOpType
ACT = mybir.ActivationFunctionType

P = 128
BATCH, SEQ, D = 16, 256, 256
TOKENS = BATCH * SEQ
BLOCK = 512
NBLK = TOKENS // BLOCK
TPB = BLOCK // P
SPB = BLOCK // SEQ
NTILE = TOKENS // P
KD = D // P
FF = 512
NEXP = 2
HT = NEXP * FF // P
DI = 512
NQ = DI // P
NH, HD = 8, 64
NS = 16
TAPS = 4
EPS = 1e-5

W_X, W_G, W_BC, W_DT, W_COLS = 0, DI, 2 * DI, 2 * DI + P, 2 * DI + P + NH
C_ROW = 32

(Q_WG, Q_B0, Q_CW, Q_CB, Q_DS, Q_NW, Q_DTB, Q_AL, Q_END) = (
    0, KD * 2, KD * 2 + HT, KD * 2 + HT + 5 * TAPS, KD * 2 + HT + 5 * TAPS + 5,
    KD * 2 + HT + 5 * TAPS + 5 + NQ, KD * 2 + HT + 5 * TAPS + 5 + 2 * NQ,
    KD * 2 + HT + 5 * TAPS + 5 + 2 * NQ + NH, KD * 2 + HT + 5 * TAPS + 5 + 2 * NQ + 2 * NH)
K_ID, K_TRI, K_SUF, K_MASK, K_NF, K_END = 0, 4 * P, 5 * P, 6 * P, 10 * P, 10 * P + 1

A_LOW, A_HIGH = 60.0, 28.7
FAST = 200.0


def macaron(nc, x, wa, wb, win, wout, params, consts, bout, out):
    ctx = ExitStack()
    with ctx:
        def sb(name, cols, dt=F32):
            return ctx.enter_context(nc.sbuf_tensor(name, [P, cols], dt))

        def sem(name):
            return ctx.enter_context(nc.semaphore(name))

        X = sb("X", NTILE * D)[:, :].rearrange("p (n d) -> p n d", d=D)
        wa_hi = sb("wa_hi", KD * HT * P, F32R)[:, :].rearrange("p (k n) -> p k n", k=KD)
        wa_lo = sb("wa_lo", KD * HT * P, F32R)[:, :].rearrange("p (k n) -> p k n", k=KD)
        wb_hi = sb("wb_hi", HT * D, F32R)[:, :].rearrange("p (k n) -> p k n", k=HT)
        wb_lo = sb("wb_lo", HT * D, F32R)[:, :].rearrange("p (k n) -> p k n", k=HT)
        wi_hi = sb("wi_hi", KD * W_COLS, F32R)[:, :].rearrange("p (k n) -> p k n", k=KD)
        wi_lo = sb("wi_lo", KD * W_COLS, F32R)[:, :].rearrange("p (k n) -> p k n", k=KD)
        wo_hi = sb("wo_hi", NQ * D, F32R)[:, :].rearrange("p (k n) -> p k n", k=NQ)
        wo_lo = sb("wo_lo", NQ * D, F32R)[:, :].rearrange("p (k n) -> p k n", k=NQ)
        wg_hi = sb("wg_hi", KD * 2, F32R)[:, :].rearrange("p (k n) -> p k n", k=KD)
        wg_lo = sb("wg_lo", KD * 2, F32R)[:, :].rearrange("p (k n) -> p k n", k=KD)
        prm = sb("prm", Q_END)
        cst = sb("cst", K_END)
        ident4 = cst[:, K_ID:K_ID + 4 * P]
        ident = cst[:, K_ID:K_ID + P]
        bo = sb("bo", 2 * D)
        xn = sb("xn", TPB * D)[:, :].rearrange("p (n d) -> p n d", d=D)
        xt_hi = sb("xt_hi", KD * BLOCK, F32R)[:, :].rearrange("p (k n) -> p k n", k=KD)
        xt_lo = sb("xt_lo", KD * BLOCK, F32R)[:, :].rearrange("p (k n) -> p k n", k=KD)
        hid_hi = sb("hid_hi", HT * BLOCK, F32R)[:, :].rearrange("p (k n) -> p k n", k=HT)
        hid_lo = sb("hid_lo", HT * BLOCK, F32R)[:, :].rearrange("p (k n) -> p k n", k=HT)
        y_hi, y_lo = hid_hi[:, 0, :], hid_lo[:, 0, :]
        n_wa, n_wb, n_wi, n_wo = KD * HT * P, HT * D, KD * W_COLS, NQ * D
        stage = sb("stage", n_wa + n_wb + n_wi + n_wo)
        st_wa = stage[:, 0:n_wa]
        st_wb = stage[:, n_wa:n_wa + n_wb]
        st_wi = stage[:, n_wa + n_wb:n_wa + n_wb + n_wi]
        st_wo = stage[:, n_wa + n_wb + n_wi:n_wa + n_wb + n_wi + n_wo]
        xs = stage[:, 0:NQ * BLOCK].rearrange("p (q n) -> p q n", q=NQ)
        gs = stage[:, NQ * BLOCK:2 * NQ * BLOCK].rearrange("p (q n) -> p q n", q=NQ)
        xd = stage[:, 2 * NQ * BLOCK:3 * NQ * BLOCK].rearrange("p (q n) -> p q n", q=NQ)
        acc = [stage[:, (3 * NQ + n) * BLOCK:(3 * NQ + n + 1) * BLOCK] for n in range(2)]
        scratch = sb("scratch", 2 * BLOCK)
        hid = raw = [scratch[:, n * BLOCK:(n + 1) * BLOCK] for n in range(2)]
        xbuf = sb("xbuf", TPB * D)
        xb = xbuf[:, :].rearrange("p (n d) -> p n d", d=D)
        xdt = [xbuf[:, n * DI:(n + 1) * DI] for n in range(2)]
        st6 = sb("st6", TPB * 6)[:, :].rearrange("p (n d) -> p n d", d=6)
        mv = sb("mv", TPB * 2)[:, :].rearrange("p (n d) -> p n d", d=2)
        mvm = sb("mvm", TPB * 2)[:, :].rearrange("p (n d) -> p n d", d=2)
        mv2 = sb("mv2", NTILE * 2)[:, :].rearrange("p (n d) -> p n d", d=2)
        veps = sb("veps", TPB)
        rstd = sb("rstd", TPB)
        rstd2 = sb("rstd2", NTILE)
        mhalf = sb("mhalf", TPB)
        logit = sb("logit", TPB * 2)[:, :].rearrange("p (n d) -> p n d", d=2)
        sel = sb("sel", TPB)
        m0h = sb("m0h", TPB)
        m1h = sb("m1h", TPB)
        ones = sb("ones", 1)
        dt_raw = sb("dt_raw", NTILE * NH)
        DEC = sb("DEC", 4 * NTILE * NH)
        dec4 = DEC[:, :].rearrange("p (k n) -> p k n", k=4)
        dec = sb("dec", 4 * TPB * NH)
        dec_b = dec[:, :].rearrange("p (k c h) -> p k c h", k=4, c=TPB)
        decay = [sb(f"decay{n}", 4 * P) for n in range(2)]
        M = sb("M", NH * P)
        yg = sb("yg", BLOCK)
        bsel = yg[:, 0:D]
        sq = sb("sq", BLOCK)
        scores = sb("scores", BLOCK)
        bt = sb("bt", BLOCK)
        part = bt[:, :].rearrange("p (n d) -> p n d", d=D)
        ct = sb("ct", BLOCK)
        bct = sb("bct", TPB * NS)
        bw = stage[:, (3 * NQ + 2) * BLOCK:(3 * NQ + 2) * BLOCK + SPB * P]
        cp = sb("cp", SPB * P)
        cpt = sb("cpt", SPB * P)
        hst = sb("hst", DI)
        yv = sb("yv", 1)
        yr = sb("yr", 1)
        eA = sb("eA", 4 * NH)

        bank = [ctx.enter_context(nc.psum_tensor(f"bank{n}", [P, 512], F32)) for n in range(8)]
        ring, l2p, l1p = bank[0:2], bank[2:4], bank[4:6]
        gatep, dtp = bank[6], bank[7]
        decp, pxp, hp, yp, op = bank[2:4], bank[4], bank[5], bank[6], bank[7]

        s_prm, s_cst, s_bo, s_wa, s_wb, s_wi, s_wo, s_out = (
            sem(n) for n in ("params_in", "consts_in", "biases_in", "wa_in", "wb_in", "wi_in", "wo_in", "stored"))
        s_x = [sem(f"x_in{n}") for n in range(NBLK)]
        w_scaled, w_hi, w_lo = sem("w_scaled"), sem("w_hi"), sem("w_lo")
        s_const, bias_half = sem("const_set"), sem("bias_half")

        def Phase(name, events):
            return {e: sem(f"{name}_{e}") for e in events}

        norm_events = ("bn", "mv", "stats", "rstd", "xn", "xt", "xhi", "xlo")
        ffn_events = norm_events + (
            "gate", "gate_read", "picked", "masks", "l1", "act", "hhi", "hlo", "l2", "xb0", "xb",
            "half", "comb", "dt", "dt_read", "mvkept")
        fa = Phase("ffn1", ffn_events)
        fb = Phase("ffn2", ffn_events)

        def dve_stats(v, f, s, blk, mvs, wait):
            wait()
            for t in range(TPB):
                ins = v.bn_stats(st6[:, t, :], X[:, blk * TPB + t, :])
            ins.then_inc(f["bn"], 1)
            v.wait_ge(f["bn"], s + 1)
            v.memset(veps[:, :], EPS)
            for t in range(TPB):
                ins = v.bn_aggr(mvs[:, t, :], st6[:, t, :])
            ins.then_inc(f["mv"], 1)
            v.wait_ge(f["mv"], s + 1)
            v.tensor_tensor(veps[:, :], veps[:, :], mvs[:, :, 1], ALU.add).then_inc(f["stats"], 1)

        def pool_rstd(g, f, s, dst):
            g.wait_ge(f["stats"], s + 1)
            g.tensor_tensor(dst, veps[:, :], mhalf[:, :], ALU.pow).then_inc(f["rstd"], 1)

        def dve_apply(v, f, s, blk, mean, rs, first):
            v.wait_ge(f["rstd"], s + 1)
            if not first:
                v.wait_ge(f["xt"], 2 * s)
            for t in range(TPB):
                ins = v.tensor_scalar(xn[:, t, :], X[:, blk * TPB + t, :], mean(t), rs(t),
                                      ALU.subtract, ALU.mult)
            ins.then_inc(f["xn"], 1)

        def pe_turn(pe, f, s, first):
            pe.wait_ge(f["xn"], s + 1)
            for k in range(KD):
                if not first:
                    pe.wait_ge(f["xlo"], 2 * s - 1 + k)
                for t in range(TPB):
                    ins = pe.transpose(ring[k][:, t * P:(t + 1) * P], xn[:, t, k * P:(k + 1) * P], ident)
                ins.then_inc(f["xt"], 1)

        def act_hi(a, f, s):
            for k in range(KD):
                a.wait_ge(f["xt"], 2 * s + k + 1)
                a.activation(xt_hi[:, k, :], ring[k][:, :], ACT.Copy).then_inc(f["xhi"], 1)

        def dve_lo(v, f, s):
            for k in range(KD):
                v.wait_ge(f["xhi"], 2 * s + k + 1)
                v.tensor_tensor(xt_lo[:, k, :], ring[k][:, :], xt_hi[:, k, :].bitcast(F32),
                                ALU.subtract).then_inc(f["xlo"], 1)

        def product(pe, dst, lhs, rhs, ks):
            ks = list(ks)
            for n, k in enumerate(ks):
                pe.matmul(dst, lhs(0, k), rhs(0, k), start=(n == 0), stop=False)
                pe.matmul(dst, lhs(0, k), rhs(1, k), start=False, stop=False)
                ins = pe.matmul(dst, lhs(1, k), rhs(0, k), start=False, stop=(n == len(ks) - 1))
            return ins

        xt = (xt_hi, xt_lo)
        wa2, wb2, wi2, wo2, wg2 = (wa_hi, wa_lo), (wb_hi, wb_lo), (wi_hi, wi_lo), (wo_hi, wo_lo), (wg_hi, wg_lo)
        hid2, y2 = (hid_hi, hid_lo), (y_hi, y_lo)

        def own(dt, i):
            return 2 * i - 1 if dt else i

        def pe_ffn(pe, f, i, dt, first, last):
            s = 0 if first else own(dt, i)
            pe.wait_ge(f["xlo"], 2 * s + 2)
            if not first:
                pe.wait_ge(f["gate_read"], i)
            for t in range(TPB):
                ins = product(pe, gatep[:, 2 * t:2 * t + 2], lambda a, k: xt[a][:, k, t * P:(t + 1) * P],
                              lambda a, k: wg2[a][:, k, :], range(KD))
            ins.then_inc(f["gate"], 1)
            for m in range(HT):
                if not (first and m < 2):
                    pe.wait_ge(f["act"], i * HT + m - 1)
                ins = product(pe, l1p[m % 2][:, :], lambda a, k: wa2[a][:, k, m * P:(m + 1) * P],
                              lambda a, k: xt[a][:, k, :], range(KD))
                ins.then_inc(f["l1"], 1)
            if dt and not first:
                pe_turn(pe, f, 2 * i, False)
            for t in range(TPB):
                if not (first and t < 2):
                    pe.wait_ge(f["comb"], i * TPB + t - 1)
                for e in range(NEXP):
                    if t == 0:
                        pe.wait_ge(f["hlo"], i * HT + 4 * e + 4)
                    ins = product(pe, l2p[t % 2][:, e * D:(e + 1) * D],
                                  lambda a, k: hid2[a][:, k, t * P:(t + 1) * P],
                                  lambda a, k: wb2[a][:, k, :], range(4 * e, 4 * e + 4))
                ins.then_inc(f["l2"], 1)
                if t == 0:
                    if dt and not first:
                        pe_dt(pe, f, 2 * i, i - 1)
                    if not last:
                        pe_turn(pe, f, own(dt, i + 1), False)

        def pe_dt(pe, f, s, b, first=False):
            pe.wait_ge(f["xlo"], 2 * s + 2)
            if not first:
                pe.wait_ge(f["dt_read"], b)
            for t in range(TPB):
                ins = product(pe, dtp[:, NH * t:NH * (t + 1)], lambda a, k: xt[a][:, k, t * P:(t + 1) * P],
                              lambda a, k: wi2[a][:, k, W_DT:W_DT + NH], range(KD))
            ins.then_inc(f["dt"], 1)

        def act_ffn(a, f, i, dt, first, last):
            for m in range(HT):
                n = i * HT + m
                a.wait_ge(f["l1"], n + 1)
                if not (first and m < 2):
                    a.wait_ge(f["hlo"], n - 1)
                func = ACT.Gelu if m < HT // NEXP else ACT.Relu
                a.activation(hid[m % 2], l1p[m % 2][:, :], func, bias=prm[:, Q_B0 + m:Q_B0 + m + 1]).then_inc(f["act"], 1)
                a.wait_ge(f["act"], n + 1)
                a.activation(hid_hi[:, m, :], hid[m % 2], ACT.Copy).then_inc(f["hhi"], 1)
            if dt and not first:
                act_hi(a, f, 2 * i)
                a.wait_ge(f["dt"], i)
            if not last:
                act_hi(a, f, own(dt, i + 1))

        def dve_ffn(v, f, i, dt, first, last):
            v.wait_ge(f["gate"], i + 1)
            v.tensor_copy(logit, gatep[:, 0:2 * TPB].rearrange("p (n d) -> p n d", d=2)).then_inc(f["gate_read"], 1)
            v.wait_ge(f["gate_read"], i + 1)
            v.tensor_tensor(sel[:, :], logit[:, :, 0], logit[:, :, 1], ALU.is_ge).then_inc(f["picked"], 1)
            v.wait_ge(f["picked"], i + 1)
            if not first:
                v.wait_ge(f["xb"], i * TPB)
            v.tensor_scalar(m0h[:, :], sel[:, :], 0.5, None, ALU.mult)
            v.tensor_scalar(m1h[:, :], sel[:, :], -0.5, 0.5, ALU.mult, ALU.add).then_inc(f["masks"], 1)

            def lo(m):
                v.wait_ge(f["hhi"], i * HT + m + 1)
                v.tensor_tensor(hid_lo[:, m, :], hid[m % 2], hid_hi[:, m, :].bitcast(F32),
                                ALU.subtract).then_inc(f["hlo"], 1)

            def combine(t):
                n = i * TPB + t
                v.wait_ge(f["l2"], n + 1)
                v.wait_ge(f["xb"], n + 1)
                v.scalar_tensor_tensor(out=part[:, t % 2, :], in0=l2p[t % 2][:, 0:D], scalar=m0h[:, t:t + 1],
                                       in1=xb[:, t, :], op0=ALU.mult, op1=ALU.add).then_inc(f["half"], 1)
                v.wait_ge(f["half"], n + 1)
                v.scalar_tensor_tensor(out=X[:, i * TPB + t, :], in0=l2p[t % 2][:, D:2 * D], scalar=m1h[:, t:t + 1],
                                       in1=part[:, t % 2, :], op0=ALU.mult, op1=ALU.add).then_inc(f["comb"], 1)

            for m in range(0, 2):
                lo(m)
            if dt and not first:
                dve_stats_mixer(v, f, i)
            for m in range(2, 4):
                lo(m)
            if dt and not first:
                dve_apply_mixer(v, f, 2 * i, i - 1)
            if not last:
                dve_stats_own(v, f, own(dt, i + 1), i + 1)
            for m in range(4, 8):
                lo(m)
            if dt and not first:
                dve_lo(v, f, 2 * i)
            if not last:
                dve_apply_own(v, f, own(dt, i + 1), i + 1)
            combine(0)
            if dt and not first:
                dve_dt_read(v, f, i - 1)
            if not last:
                dve_lo(v, f, own(dt, i + 1))
            for t in range(1, TPB):
                combine(t)

        def dve_stats_own(v, f, s, blk, first=False):
            def there():
                if f is fa:
                    if isinstance(blk, int):
                        v.wait_ge(s_x[blk], 16)
                    else:
                        for n in range(NBLK):
                            v.wait_ge(s_x[n], 16)
                else:
                    v.wait_ge(mx["fin"], NTILE)
            dve_stats(v, f, s, blk, mv, there)

        def dve_apply_own(v, f, s, blk, first=False):
            dve_apply(v, f, s, blk, lambda t: mv[:, t, 0:1], lambda t: rstd[:, t:t + 1], first)

        def dve_stats_mixer(v, f, i, s=None):
            b = i - 1
            dve_stats(v, f, 2 * i if s is None else s, b, mvm,
                      lambda: v.wait_ge(f["comb"], i * TPB))
            v.tensor_copy(mv2[:, bass.ds(b * TPB, TPB), :], mvm[:, :, :]).then_inc(f["mvkept"], 1)

        def dve_apply_mixer(v, f, s, b, first=False):
            v.wait_ge(f["mvkept"], b + 1)
            dve_apply(v, f, s, b, lambda t: mv2[:, b * TPB + t, 0:1],
                      lambda t: rstd2[:, bass.ds(b * TPB + t, 1)], first)

        def dve_dt_read(v, f, b):
            v.wait_ge(f["dt"], b + 1)
            v.tensor_copy(dt_raw[:, bass.ds(b * TPB * NH, TPB * NH)], dtp[:, 0:TPB * NH]).then_inc(f["dt_read"], 1)

        def pool_ffn(g, f, i, dt, first, last):
            if dt and not first:
                pool_rstd(g, f, 2 * i, rstd2[:, bass.ds((i - 1) * TPB, TPB)])
            if not last:
                pool_rstd(g, f, own(dt, i + 1), rstd[:, :])
            g.wait_ge(f["masks"], i + 1)
            for t in range(TPB):
                n = i * TPB + t
                if not first:
                    g.wait_ge(f["comb"], n - TPB + 1)
                if not (first and t == 0):
                    g.wait_ge(f["xb"], n)
                g.tensor_tensor(xb[:, t, :], X[:, i * TPB + t, :], bo[:, D:2 * D], ALU.add)
                g.tensor_scalar(bsel, bo[:, 0:D], m0h[:, t:t + 1], None, ALU.mult).then_inc(f["xb0"], 1)
                g.wait_ge(f["xb0"], n + 1)
                g.tensor_tensor(xb[:, t, :], xb[:, t, :], bsel, ALU.add).then_inc(f["xb"], 1)

        def blocks(eng, step):
            step(0, True, False)
            with eng.Fori(1, NBLK - 1) as i:
                step(i, False, False)
            step(NBLK - 1, False, True)

        mx = Phase("mix", ("xn", "xhi",
            "full0", "full1", "free0", "free1", "dec", "tap", "silu", "bcsilu", "xd", "bwcp", "px", "xdt", "decp",
            "scan", "mm", "hp", "hst", "yp", "ysum", "yg", "sq", "yhi", "ylo", "op", "yv", "yr", "fin"))
        full, free = (mx["full0"], mx["full1"]), (mx["free0"], mx["free1"])
        SLOTS = ["x1", "x2", "x3", "g0", "g1", "S", "BCT", "g2", "CPT", "g3", "T0", "T1", "BC", "x0"]
        PER = len(SLOTS) // 2

        def slot(i, what, ahead=False):
            j = SLOTS.index(what)
            if ahead:
                return j % 2, i * PER + (j - 10) // 2
            return j % 2, i * PER + 2 + j // 2

        def fill(pe, sl, first=False):
            b, n = sl
            if not first:
                pe.wait_ge(free[b], n)
            return ring[b], full[b]

        def filled(eng, sl):
            b, n = sl
            eng.wait_ge(full[b], n + 1)
            return ring[b], free[b]

        def emptied(eng, sl):
            b, n = sl
            eng.wait_ge(free[b], n + 1)

        def pe_inproj(pe, sl, col, first=False):
            dst, done = fill(pe, sl, first)
            product(pe, dst[:, :], lambda a, k: wi2[a][:, k, col:col + P],
                    lambda a, k: xt[a][:, k, :], range(KD)).then_inc(done, 1)

        def pe_mix_ahead(pe, i, first):
            pe.wait_ge(mx["xn"], i + 1)
            for k in range(KD):
                dst, done = fill(pe, slot(i, f"T{k}", True), first)
                for t in range(TPB):
                    ins = pe.transpose(dst[:, t * P:(t + 1) * P], xn[:, t, k * P:(k + 1) * P], ident)
                ins.then_inc(done, 1)

        def pe_mix_ahead2(pe, i):
            for k in range(KD):
                emptied(pe, slot(i, f"T{k}", True))
            pe_inproj(pe, slot(i, "BC", True), W_BC)
            pe_inproj(pe, slot(i, "x0", True), W_X)

        def pe_decay(pe, i, c, first):
            for half in range(2):
                if not (first and c == 0):
                    pe.wait_ge(mx["scan"], (i * TPB + c) * 2 + half - 1)
                if c == 0 and half == 0:
                    pe.wait_ge(mx["dec"], i + 1)
                for h in range(4):
                    ins = pe.transpose(decp[half][:, h * P:(h + 1) * P],
                                       dec_b[:, 0, c, 4 * half + h:4 * half + h + 1].broadcast_to([P, P]), ident)
                ins.then_inc(mx["decp"], 1)

        def pe_px(pe, i, c, first):
            if c == 0:
                pe.wait_ge(mx["silu"], (i + 1) * NQ)
            if not (first and c == 0):
                pe.wait_ge(mx["xdt"], i * TPB + c)
            for q in range(NQ):
                ins = pe.transpose(pxp[:, q * P:(q + 1) * P], xs[:, q, c * P:(c + 1) * P], ident)
            ins.then_inc(mx["px"], 1)

        def pe_state(pe, i, s, first):
            c = 2 * s
            pe.wait_ge(mx["xdt"], i * TPB + c + 1)
            if s == 0:
                pe.wait_ge(mx["bwcp"], i + 1)
            if not (first and s == 0):
                pe.wait_ge(mx["hst"], i * SPB + s)
            pe.matmul(hp[:, :], bw[:, s * P:(s + 1) * P], xdt[c % 2], start=True, stop=True).then_inc(mx["hp"], 1)

        def pe_y(pe, i, c, first):
            n = i * TPB + c
            pe.wait_ge(mx["xdt"], n + 1)
            pe.wait_ge(mx["mm"], 2 * n + 2)
            if not (first and c == 0):
                pe.wait_ge(mx["ysum"], n)
            if c % 2:
                pe.wait_ge(mx["hst"], i * SPB + c // 2 + 1)
                emptied(pe, slot(i, "CPT"))
            for q in range(NQ):
                if c % 2:
                    pe.matmul(yp[:, q * P:(q + 1) * P], hst[:, q * P:(q + 1) * P],
                              cpt[:, (c // 2) * P:(c // 2 + 1) * P], start=True, stop=False, skip_group_check=True)
                for h in range(2):
                    ins = pe.matmul(yp[h * HD:(h + 1) * HD, q * P:(q + 1) * P],
                                    xdt[c % 2][:, (2 * q + h) * HD:(2 * q + h + 1) * HD],
                                    M[:, (2 * q + h) * P:(2 * q + h + 1) * P],
                                    start=(c % 2 == 0), stop=True, skip_group_check=True)
            ins.then_inc(mx["yp"], 1)

        def pe_out(pe, i, c, first):
            n = i * TPB + c
            if not (first and c == 0):
                pe.wait_ge(mx["fin"], n)
            pe.wait_ge(mx["sq"], n + 1)
            for q in range(NQ):
                pe.matmul(op[:, D:D + 1], sq[:, q * P:(q + 1) * P], ones[:, :], start=(q == 0), stop=(q == NQ - 1))
            pe.wait_ge(mx["ylo"], n + 1)
            product(pe, op[:, 0:D], lambda a, k: y2[a][:, k * P:(k + 1) * P],
                    lambda a, k: wo2[a][:, k, :], range(NQ)).then_inc(mx["op"], 1)

        def pe_mix(pe, i, first, last):
            for q in range(1, NQ):
                pe_inproj(pe, slot(i, f"x{q}"), W_X + q * P)
            pe_decay(pe, i, 0, first)
            for q in range(2):
                pe_inproj(pe, slot(i, f"g{q}"), W_G + q * P)
            dst, done = fill(pe, slot(i, "S"))
            dst_t, done_t = fill(pe, slot(i, "BCT"))
            pe.wait_ge(mx["bcsilu"], i + 1)
            for c in range(TPB):
                ins = pe.matmul(dst[:, c * P:(c + 1) * P], bt[0:NS, c * P:(c + 1) * P], ct[0:NS, c * P:(c + 1) * P],
                                start=True, stop=True)
            ins.then_inc(done, 1)
            for c in range(TPB):
                src = ct if c % 2 else bt
                ins = pe.transpose(dst_t[:, c * NS:(c + 1) * NS], src[0:NS, c * P:(c + 1) * P], ident[0:NS, 0:NS])
            ins.then_inc(done_t, 1)
            pe_inproj(pe, slot(i, "g2"), W_G + 2 * P)
            dst, done = fill(pe, slot(i, "CPT"))
            pe.wait_ge(mx["bwcp"], i + 1)
            for s in range(SPB):
                ins = pe.transpose(dst[:, s * P:(s + 1) * P], cp[:, s * P:(s + 1) * P], ident)
            ins.then_inc(done, 1)
            pe_inproj(pe, slot(i, "g3"), W_G + 3 * P)
            pe_px(pe, i, 0, first)
            for c in range(TPB):
                if c % 2 == 0:
                    pe_state(pe, i, c // 2, first)
                if c + 1 < TPB:
                    pe_px(pe, i, c + 1, first)
                    pe_decay(pe, i, c + 1, first)
                elif not last:
                    pe_mix_ahead(pe, i + 1, False)
                pe_y(pe, i, c, first)
                if c:
                    pe_out(pe, i, c - 1, first)
            if not last:
                pe_mix_ahead2(pe, i + 1)
            pe_out(pe, i, TPB - 1, first)

        def conv_rows(n):
            return slice(0, C_ROW + NS) if n == 0 else slice(0, P)

        def act_raw(a, i, n, sl, first):
            src, done = filled(a, sl)
            r = conv_rows(n)
            prev = (5 * i - 1, 5 * i - 2, 5 * i, 5 * i + 1, 5 * i + 2)[n]
            if not (first and n < 2):
                a.wait_ge(mx["tap"], 3 * (prev + 1))
                if n == 2:
                    a.wait_ge(mx["bcsilu"], i + 1)
                else:
                    a.wait_ge(mx["silu"], i * NQ + max(n - 2, 0))
            cw = Q_CW + n * TAPS
            a.activation(raw[n % 2][r, :], src[r, :], ACT.Copy)
            a.activation(acc[n % 2][r, :], src[r, :], ACT.Identity, bias=prm[r, Q_CB + n:Q_CB + n + 1],
                         scale=prm[r, cw + 3:cw + 4]).then_inc(done, 1)

        def dve_conv(v, i, n):
            emptied(v, slot(i, ("BC", "x0", "x1", "x2", "x3")[n], n < 2))
            r = conv_rows(n)
            rows = raw[n % 2][r, :].rearrange("p (s t) -> p s t", s=SPB)
            accs = acc[n % 2][r, :].rearrange("p (s t) -> p s t", s=SPB)
            cw = Q_CW + n * TAPS
            for back in range(1, TAPS):
                if back > 1:
                    v.wait_ge(mx["tap"], 3 * (5 * i + n) + back - 1)
                v.scalar_tensor_tensor(out=accs[:, :, back:], in0=rows[:, :, 0:SEQ - back],
                                       scalar=prm[r, cw + 3 - back:cw + 4 - back], in1=accs[:, :, back:],
                                       op0=ALU.mult, op1=ALU.add).then_inc(mx["tap"], 1)

        def act_silu_bc(a, i, first):
            a.wait_ge(mx["tap"], 3 * (5 * i) + 3)
            a.activation(bt[0:NS, :], acc[0][0:NS, :], ACT.Silu)
            a.activation(ct[0:NS, :], acc[0][C_ROW:C_ROW + NS, :], ACT.Silu).then_inc(mx["bcsilu"], 1)

        def act_silu_x(a, i, q, first):
            n = 1 + q
            a.wait_ge(mx["tap"], 3 * (5 * i + n) + 3)
            if not first and q == 0:
                a.wait_ge(mx["px"], i * TPB)
            a.activation(xs[:, q, :], acc[n % 2], ACT.Silu).then_inc(mx["silu"], 1)

        def act_xd(a, i, q, first):
            if not first and q == 0:
                a.wait_ge(mx["ysum"], i * TPB)
            a.wait_ge(mx["silu"], i * NQ + q + 1)
            a.activation(xd[:, q, :], xs[:, q, :], ACT.Copy, scale=prm[:, Q_DS + q:Q_DS + q + 1]).then_inc(mx["xd"], 1)

        def act_gate(a, i, q, first):
            src, done = filled(a, slot(i, f"g{q}"))
            if not first and q == 0:
                a.wait_ge(mx["yg"], i * TPB)
            a.activation(gs[:, q, :], src[:, :], ACT.Silu).then_inc(done, 1)

        def act_copy(a, i, what, dst, cols, wait):
            src, done = filled(a, slot(i, what))
            wait()
            a.activation(dst, src[:, 0:cols], ACT.Copy).then_inc(done, 1)

        def act_out(a, i, c, first):
            n = i * TPB + c
            a.wait_ge(mx["yg"], n + 1)
            if not (first and c == 0):
                a.wait_ge(mx["op"], n)
            a.activation(sq[:, :], yg[:, :], ACT.Square).then_inc(mx["sq"], 1)
            a.activation(y_hi[:, :], yg[:, :], ACT.Copy).then_inc(mx["yhi"], 1)

        def act_mix_ahead(a, i, first):
            for k in range(KD):
                src, _ = filled(a, slot(i, f"T{k}", True))
                if k == 0 and not first:
                    b, n = slot(i - 1, "g3")
                    a.wait_ge(full[b], n + 1)
                a.activation(xt_hi[:, k, :], src[:, :], ACT.Copy).then_inc(mx["xhi"], 1)

        def dve_mix_ahead(v, i):
            for k in range(KD):
                v.wait_ge(mx["xhi"], 2 * i + k + 1)
                b, _ = slot(i, f"T{k}", True)
                v.tensor_tensor(xt_lo[:, k, :], ring[b][:, :], xt_hi[:, k, :].bitcast(F32),
                                ALU.subtract).then_inc(free[b], 1)

        def act_mix(a, i, first, last):
            act_silu_bc(a, i, first)
            act_raw(a, i, 2, slot(i, "x1"), first)
            act_silu_x(a, i, 0, first)
            act_raw(a, i, 3, slot(i, "x2"), first)
            act_silu_x(a, i, 1, first)
            act_raw(a, i, 4, slot(i, "x3"), first)
            act_gate(a, i, 0, first)
            act_gate(a, i, 1, first)

            def scores_free():
                if not first:
                    a.wait_ge(mx["mm"], i * TPB * 2)
            act_copy(a, i, "S", scores[:, :], BLOCK, scores_free)

            def bct_free():
                if not first:
                    a.wait_ge(mx["bwcp"], i)
            act_copy(a, i, "BCT", bct[:, :], TPB * NS, bct_free)
            act_silu_x(a, i, 2, first)
            act_gate(a, i, 2, first)
            act_silu_x(a, i, 3, first)

            def cpt_free():
                if not first:
                    a.wait_ge(mx["yp"], i * TPB)
            act_copy(a, i, "CPT", cpt[:, :], SPB * P, cpt_free)
            act_gate(a, i, 3, first)
            for q in range(NQ):
                act_xd(a, i, q, first)
            for c in range(TPB - 1):
                act_out(a, i, c, first)
            if not last:
                act_mix_ahead(a, i + 1, False)
            act_out(a, i, TPB - 1, first)
            if not last:
                act_raw(a, i + 1, 0, slot(i + 1, "BC", True), False)
                act_raw(a, i + 1, 1, slot(i + 1, "x0", True), False)

        def dve_scan(v, i, c, first):
            for half in range(2):
                n = (i * TPB + c) * 2 + half
                v.wait_ge(mx["decp"], n + 1)
                if not (first and c == 0):
                    v.wait_ge(mx["mm"], n - 1)
                v.tensor_tensor_scan(decay[half][:, :], decp[half][:, :], ident4, 0.0,
                                     ALU.mult, ALU.add).then_inc(mx["scan"], 1)

        def dve_matrix(v, i, c, first):
            for half in range(2):
                n = (i * TPB + c) * 2 + half
                v.wait_ge(mx["scan"], n + 1)
                if half == 0:
                    emptied(v, slot(i, "S"))
                    if not (first and c == 0):
                        v.wait_ge(mx["yp"], i * TPB + c)
                v.tensor_tensor(M[:, half * 4 * P:(half + 1) * 4 * P].rearrange("p (h t) -> p h t", h=4),
                                decay[half][:, :].rearrange("p (h t) -> p h t", h=4),
                                scores[:, c * P:(c + 1) * P].unsqueeze(1).broadcast_to([P, 4, P]),
                                ALU.mult).then_inc(mx["mm"], 1)

        def dve_xdt(v, i, c, first):
            n = i * TPB + c
            v.wait_ge(mx["px"], n + 1)
            if not (first and c < 2):
                v.wait_ge(mx["yp"], n - 1)
            v.tensor_tensor(xdt[c % 2].rearrange("p (h d) -> p h d", h=NH),
                            pxp[:, :].rearrange("p (h d) -> p h d", h=NH),
                            dec_b[:, 1, c, :].unsqueeze(2).broadcast_to([P, NH, HD]), ALU.mult).then_inc(mx["xdt"], 1)

        def dve_scaled_bc(v, i, first):
            emptied(v, slot(i, "BCT"))
            if not first:
                v.wait_ge(mx["hp"], i * SPB)
            for s in range(SPB):
                for dst, c, kind in ((bw, 2 * s, 3), (cp, 2 * s + 1, 2)):
                    ins = v.tensor_tensor(dst[:, s * P:(s + 1) * P].rearrange("p (h n) -> p h n", h=NH),
                                          bct[:, c * NS:(c + 1) * NS].unsqueeze(1).broadcast_to([P, NH, NS]),
                                          dec_b[:, kind, c, :].unsqueeze(2).broadcast_to([P, NH, NS]), ALU.mult)
            ins.then_inc(mx["bwcp"], 1)

        def dve_state(v, i, s, first):
            v.wait_ge(mx["hp"], i * SPB + s + 1)
            if not (first and s == 0):
                v.wait_ge(mx["yp"], i * TPB + 2 * s)
            v.tensor_tensor(hst[:, :], hp[:, :], cst[:, K_MASK:K_MASK + DI], ALU.mult).then_inc(mx["hst"], 1)

        def dve_y(v, i, c, first):
            n = i * TPB + c
            v.wait_ge(mx["yp"], n + 1)
            if c == 0:
                v.wait_ge(mx["xd"], (i + 1) * NQ)
            if not (first and c == 0):
                v.wait_ge(mx["yhi"], n)
                v.wait_ge(mx["ylo"], n)
            here = slice(c * P, (c + 1) * P)
            y4 = yg[:, :].rearrange("p (q t) -> p q t", q=NQ)
            v.tensor_tensor(y4, yp[:, :].rearrange("p (q t) -> p q t", q=NQ), xd[:, :, here],
                            ALU.add).then_inc(mx["ysum"], 1)
            v.wait_ge(mx["ysum"], n + 1)
            if c == 0:
                emptied(v, slot(i, "g3"))
            v.tensor_tensor(y4, y4, gs[:, :, here], ALU.mult).then_inc(mx["yg"], 1)
            v.wait_ge(mx["yhi"], n + 1)
            v.tensor_tensor(y_lo[:, :], yg[:, :], y_hi[:, :].bitcast(F32), ALU.subtract).then_inc(mx["ylo"], 1)

        def dve_final_scale(v, i, c, first):
            n = i * TPB + c
            v.wait_ge(mx["op"], n + 1)
            v.tensor_scalar(yv[:, :], op[:, D:D + 1], 1.0 / DI, EPS, ALU.mult, ALU.add).then_inc(mx["yv"], 1)

        def dve_final(v, i, c):
            n = i * TPB + c
            v.wait_ge(mx["yr"], n + 1)
            v.scalar_tensor_tensor(out=X[:, n, :], in0=op[:, 0:D], scalar=yr[:, :], in1=X[:, n, :],
                                   op0=ALU.mult, op1=ALU.add).then_inc(mx["fin"], 1)

        def pool_mix(g, i, first, last):
            for c in range(TPB):
                n = i * TPB + c
                g.wait_ge(mx["yv"], n + 1)
                g.tensor_tensor(yr[:, :], yv[:, :], mhalf[:, 0:1], ALU.pow).then_inc(mx["yr"], 1)

        def dve_dec(v, i, first):
            if not first:
                v.wait_ge(mx["bwcp"], i)
                v.wait_ge(mx["decp"], i * TPB * 2)
            v.tensor_copy(dec[:, :].rearrange("p (k n) -> p k n", k=4),
                          dec4[:, :, bass.ds(i * TPB * NH, TPB * NH)]).then_inc(mx["dec"], 1)
            v.wait_ge(mx["dec"], i + 1)

        def dve_mix_xn(v, i, first):
            if not first:
                filled(v, slot(i - 1, "T1", True))
            for t in range(TPB):
                ins = v.tensor_scalar(xn[:, t, :], X[:, i * TPB + t, :], mv2[:, i * TPB + t, 0:1],
                                      rstd2[:, bass.ds(i * TPB + t, 1)], ALU.subtract, ALU.mult)
            ins.then_inc(mx["xn"], 1)

        def dve_mix(v, i, first, last):
            dve_dec(v, i, first)
            dve_conv(v, i, 0)
            dve_conv(v, i, 1)
            dve_conv(v, i, 2)
            dve_scan(v, i, 0, first)
            dve_conv(v, i, 3)
            dve_scaled_bc(v, i, first)
            dve_conv(v, i, 4)
            if not last:
                dve_mix_xn(v, i + 1, False)
            dve_matrix(v, i, 0, first)
            dve_xdt(v, i, 0, first)
            for c in range(TPB):
                if c + 1 < TPB:
                    dve_xdt(v, i, c + 1, first)
                    dve_scan(v, i, c + 1, first)
                if c % 2 == 0:
                    dve_state(v, i, c // 2, first)
                if c == TPB - 1 and not last:
                    dve_mix_ahead(v, i + 1)
                dve_y(v, i, c, first)
                if c + 1 < TPB:
                    dve_matrix(v, i, c + 1, first)
                if c:
                    dve_final_scale(v, i, c - 1, first)
                    dve_final(v, i, c - 1)
            dve_final_scale(v, i, TPB - 1, first)
            dve_final(v, i, TPB - 1)

        tail = Phase("dt", ("v", "av", "e", "u", "ln", "um1", "z", "den", "rec", "q", "q2", "ez", "dt0", "dt",
                            "clip", "eA", "a1", "a2", "a3", "a", "dA", "cum", "P", "done"))
        NA = NTILE * NH
        tmp = [stage[:, n * NA:(n + 1) * NA] for n in range(8)]
        t_v, t_a, t_e, t_u, t_l, t_z, t_r, t_q = tmp
        dt_all, dA_all = dec4[:, 1, :], dec4[:, 0, :]

        def per_head(col):
            return eA[:, col * NH:(col + 1) * NH].unsqueeze(1).broadcast_to([P, NTILE, NH])

        def by_head(ap):
            return ap.rearrange("p (n h) -> p n h", h=NH)

        def dve_tail(v):
            def step(ins, s):
                ins.then_inc(s, 1)
                v.wait_ge(s, 1)

            v.wait_ge(fa["dt_read"], NBLK)
            step(v.tensor_tensor(by_head(t_v), by_head(dt_raw[:, :]),
                                 prm[:, Q_DTB:Q_DTB + NH].unsqueeze(1).broadcast_to([P, NTILE, NH]), ALU.add), tail["v"])
            step(v.scalar_tensor_tensor(out=t_a, in0=t_v, scalar=-1.0, in1=t_v, op0=ALU.mult, op1=ALU.max), tail["av"])
            v.tensor_scalar(eA[:, 0:NH], prm[:, Q_AL:Q_AL + NH], A_LOW, None, ALU.min)
            step(v.tensor_scalar(eA[:, NH:2 * NH], prm[:, Q_AL:Q_AL + NH], A_LOW, 0.0, ALU.subtract, ALU.max), tail["clip"])
            v.tensor_scalar(eA[:, NH:2 * NH], eA[:, NH:2 * NH], A_HIGH, None, ALU.min).then_inc(tail["clip"], 1)
            v.wait_ge(tail["e"], 1)
            step(v.tensor_scalar(t_u, t_e, 1.0, None, ALU.add), tail["u"])
            step(v.tensor_scalar(t_r, t_u, 1.0, None, ALU.subtract), tail["um1"])
            step(v.tensor_scalar(t_z, t_r, 0.0, None, ALU.is_equal), tail["z"])
            step(v.tensor_tensor(t_r, t_r, t_z, ALU.add), tail["den"])
            step(v.reciprocal(t_r, t_r), tail["rec"])
            v.wait_ge(tail["ln"], 1)
            step(v.tensor_tensor(t_q, t_l, t_e, ALU.mult), tail["q"])
            step(v.tensor_tensor(t_q, t_q, t_r, ALU.mult), tail["q2"])
            step(v.tensor_tensor(t_z, t_z, t_e, ALU.mult), tail["ez"])
            step(v.tensor_tensor(t_q, t_q, t_z, ALU.add), tail["dt0"])
            step(v.scalar_tensor_tensor(out=dt_all, in0=t_v, scalar=0.0, in1=t_q, op0=ALU.max, op1=ALU.add), tail["dt"])
            v.wait_ge(tail["eA"], 1)
            step(v.tensor_tensor(by_head(t_a), by_head(dt_all), per_head(2), ALU.mult), tail["a1"])
            step(v.tensor_scalar(t_a, t_a, FAST, None, ALU.min), tail["a2"])
            step(v.tensor_tensor(by_head(t_a), by_head(t_a), per_head(3), ALU.mult), tail["a3"])
            step(v.tensor_scalar(t_a, t_a, FAST, None, ALU.min), tail["a"])
            v.wait_ge(tail["dA"], 1)
            v.tensor_scalar(dA_all, t_u, cst[:, K_NF:K_NF + 1], None, ALU.mult).then_inc(tail["done"], 1)
            v.wait_ge(tail["P"], 2)
            v.wait_ge(tail["done"], 1)

        def act_tail(a):
            a.wait_ge(tail["av"], 1)
            a.activation(t_e, t_a, ACT.Exp, scale=-1.0).then_inc(tail["e"], 1)
            a.wait_ge(tail["clip"], 2)
            a.activation(eA[:, 2 * NH:4 * NH], eA[:, 0:2 * NH], ACT.Exp).then_inc(tail["eA"], 1)
            a.wait_ge(tail["u"], 1)
            a.activation(t_l, t_u, ACT.Ln).then_inc(tail["ln"], 1)
            a.wait_ge(tail["a"], 1)
            a.wait_ge(tail["um1"], 1)
            a.activation(t_u, t_a, ACT.Exp, scale=-1.0).then_inc(tail["dA"], 1)
            a.wait_ge(tail["cum"], 1)
            a.activation(dec4[:, 2, :], yp[:, 0:NA], ACT.Exp, scale=-1.0).then_inc(tail["P"], 1)
            a.activation(dec4[:, 3, :], yp[:, NA:2 * NA], ACT.Exp, scale=-1.0).then_inc(tail["P"], 1)

        def pe_tail(pe):
            pe.wait_ge(tail["a"], 1)
            pe.matmul(yp[:, 0:NA], cst[:, K_TRI:K_TRI + P], t_a, start=True, stop=True)
            pe.matmul(yp[:, NA:2 * NA], cst[:, K_SUF:K_SUF + P], t_a, start=True, stop=True).then_inc(tail["cum"], 1)

        block = ctx.enter_context(nc.Block())

        @block.sync
        def _(sp):
            xv = x.rearrange("(i t p) d -> i p t d", t=TPB, p=P)
            ov = out.rearrange("(i t p) d -> i p t d", t=TPB, p=P)
            sp.dma_start(X[:, 0:TPB, :], xv[0]).then_inc(s_x[0], 16)
            sp.dma_start(prm[:, :], params).then_inc(s_prm, 16)
            sp.dma_start(cst[:, :], consts).then_inc(s_cst, 16)
            sp.dma_start(st_wa, wa).then_inc(s_wa, 16)
            sp.dma_start(X[:, TPB:2 * TPB, :], xv[1]).then_inc(s_x[1], 16)
            sp.dma_start(st_wb, wb).then_inc(s_wb, 16)
            sp.dma_start(bo[:, :], bout).then_inc(s_bo, 16)
            sp.dma_start(st_wi, win).then_inc(s_wi, 16)
            sp.dma_start(st_wo, wout).then_inc(s_wo, 16)
            for n in range(2, NBLK):
                sp.dma_start(X[:, n * TPB:(n + 1) * TPB, :], xv[n]).then_inc(s_x[n], 16)
            with sp.Fori(0, NBLK) as i:
                sp.wait_ge(fb["comb"], i * TPB + TPB)
                sp.dma_start(ov[i], X[:, bass.ds(i * TPB, TPB), :]).then_inc(s_out, 16)
            sp.wait_ge(s_out, 16 * NBLK)

        @block.gpsimd
        def _(g):
            g.memset(mhalf[:, :], -0.5).then_inc(s_const, 1)
            g.memset(ones[:, :], 1.0).then_inc(s_const, 1)
            g.wait_ge(s_const, 2)
            pool_rstd(g, fa, 0, rstd[:, :])
            g.wait_ge(bias_half, 2)
            blocks(g, lambda i, first, last: pool_ffn(g, fa, i, True, first, last))
            pool_rstd(g, fa, 2 * NBLK - 1, rstd2[:, (NBLK - 1) * TPB:NTILE])
            blocks(g, lambda i, first, last: pool_mix(g, i, first, last))
            pool_rstd(g, fb, 0, rstd[:, :])
            blocks(g, lambda i, first, last: pool_ffn(g, fb, i, False, first, last))

        @block.scalar
        def _(a):
            def hi(dst, src, wait):
                wait()
                a.activation(dst.rearrange("p k n -> p (k n)"), src, ACT.Copy).then_inc(w_hi, 1)

            hi(wg_hi, prm[:, Q_WG:Q_WG + KD * 2], lambda: a.wait_ge(s_prm, 16))
            hi(wa_hi, st_wa, lambda: a.wait_ge(s_wa, 16))
            act_hi(a, fa, 0)
            hi(wb_hi, st_wb, lambda: a.wait_ge(s_wb, 16))
            hi(wi_hi, st_wi, lambda: a.wait_ge(s_wi, 16))
            hi(wo_hi, st_wo, lambda: a.wait_ge(w_scaled, 1))
            blocks(a, lambda i, first, last: act_ffn(a, fa, i, True, first, last))
            act_hi(a, fa, 2 * NBLK - 1)
            act_tail(a)
            act_mix_ahead(a, 0, True)
            act_raw(a, 0, 0, slot(0, "BC", True), True)
            act_raw(a, 0, 1, slot(0, "x0", True), True)
            blocks(a, lambda i, first, last: act_mix(a, i, first, last))
            act_hi(a, fb, 0)
            blocks(a, lambda i, first, last: act_ffn(a, fb, i, False, first, last))

        @block.vector
        def _(v):
            def lo(dst, hi, src, n):
                v.wait_ge(w_hi, n + 1)
                v.tensor_tensor(dst.rearrange("p k n -> p (k n)"), src,
                                hi.rearrange("p k n -> p (k n)").bitcast(F32), ALU.subtract).then_inc(w_lo, 1)

            dve_stats_own(v, fa, 0, 0)
            v.wait_ge(s_prm, 16)
            lo(wg_lo, wg_hi, prm[:, Q_WG:Q_WG + KD * 2], 0)
            dve_apply_own(v, fa, 0, 0, True)
            lo(wa_lo, wa_hi, st_wa, 1)
            dve_lo(v, fa, 0)
            v.wait_ge(s_wo, 16)
            for q in range(NQ):
                ins = v.tensor_scalar(st_wo[:, q * D:(q + 1) * D], st_wo[:, q * D:(q + 1) * D],
                                      prm[:, Q_NW + q:Q_NW + q + 1], None, ALU.mult)
            ins.then_inc(w_scaled, 1)
            v.wait_ge(s_bo, 16)
            v.tensor_tensor(bo[:, 0:D], bo[:, 0:D], bo[:, D:2 * D], ALU.subtract).then_inc(bias_half, 1)
            v.wait_ge(bias_half, 1)
            v.tensor_scalar(bo[:, D:2 * D], bo[:, D:2 * D], 0.5, None, ALU.mult).then_inc(bias_half, 1)
            lo(wb_lo, wb_hi, st_wb, 2)
            lo(wi_lo, wi_hi, st_wi, 3)
            v.wait_ge(w_scaled, 1)
            lo(wo_lo, wo_hi, st_wo, 4)
            blocks(v, lambda i, first, last: dve_ffn(v, fa, i, True, first, last))
            dve_stats_mixer(v, fa, NBLK, 2 * NBLK - 1)
            dve_apply_mixer(v, fa, 2 * NBLK - 1, NBLK - 1)
            dve_lo(v, fa, 2 * NBLK - 1)
            dve_dt_read(v, fa, NBLK - 1)
            dve_mix_xn(v, 0, True)
            dve_tail(v)
            dve_mix_ahead(v, 0)
            blocks(v, lambda i, first, last: dve_mix(v, i, first, last))
            dve_stats_own(v, fb, 0, 0)
            dve_apply_own(v, fb, 0, 0, True)
            dve_lo(v, fb, 0)
            blocks(v, lambda i, first, last: dve_ffn(v, fb, i, False, first, last))

        @block.tensor
        def _(pe):
            pe.wait_ge(s_cst, 16)
            pe_turn(pe, fa, 0, True)
            pe.wait_ge(w_lo, 5)
            pe.wait_ge(s_const, 2)
            blocks(pe, lambda i, first, last: pe_ffn(pe, fa, i, True, first, last))
            pe_turn(pe, fa, 2 * NBLK - 1, False)
            pe_dt(pe, fa, 2 * NBLK - 1, NBLK - 1)
            pe.wait_ge(fa["dt_read"], NBLK)
            pe_tail(pe)
            pe_mix_ahead(pe, 0, True)
            pe_mix_ahead2(pe, 0)
            pe.wait_ge(tail["P"], 2)
            blocks(pe, lambda i, first, last: pe_mix(pe, i, first, last))
            pe.wait_ge(mx["fin"], NTILE)
            pe_turn(pe, fb, 0, True)
            blocks(pe, lambda i, first, last: pe_ffn(pe, fb, i, False, first, last))


def kernel(**inputs):
    import numpy as np
    import concourse.bacc as bacc
    from concourse.bass_utils import run_bass_kernel_spmd

    a = {n.replace("L0_", ""): np.asarray(v) for n, v in inputs.items()}
    f = np.float32

    def tiles(w, k):
        return np.ascontiguousarray(w.reshape(k, P, -1).transpose(1, 0, 2).reshape(P, -1))

    def rows(v):
        return np.broadcast_to(v.reshape(1, -1), (P, v.size))

    wa = tiles(np.concatenate([a["ffn_W0a"], a["ffn_W1a"]]).T, KD)
    wb = tiles(np.concatenate([a["ffn_W0b"].T, a["ffn_W1b"].T]), HT)
    w = a["attn_W_in"]
    wi = np.zeros((D, W_COLS), f)
    wi[:, W_X:W_X + DI] = w[:, DI:2 * DI]
    wi[:, W_G:W_G + DI] = w[:, 0:DI]
    wi[:, W_BC:W_BC + NS] = w[:, 2 * DI:2 * DI + NS]
    wi[:, W_BC + C_ROW:W_BC + C_ROW + NS] = w[:, 2 * DI + NS:2 * DI + 2 * NS]
    wi[:, W_DT:W_DT + NH] = w[:, 2 * DI + 2 * NS:]
    win = tiles(wi, KD)
    wout = tiles(a["attn_W_out"], NQ)

    prm = np.zeros((P, Q_END), f)
    prm[:, Q_WG:Q_WG + 2 * KD] = tiles(a["ffn_Wg"].T, KD)
    prm[:, Q_B0:Q_B0 + HT] = np.concatenate([a["ffn_b0a"], a["ffn_b1a"]]).reshape(HT, P).T
    cw, cb = a["attn_conv_w"], a["attn_conv_b"]
    for n in range(5):
        for at, lo, hi in ([(0, DI, DI + NS), (C_ROW, DI + NS, DI + 2 * NS)] if n == 0 else
                           [(0, (n - 1) * P, n * P)]):
            prm[at:at + hi - lo, Q_CW + n * TAPS:Q_CW + (n + 1) * TAPS] = cw[lo:hi]
            prm[at:at + hi - lo, Q_CB + n] = cb[lo:hi]
    prm[:, Q_DS:Q_DS + NQ] = np.repeat(a["attn_D_skip"], HD).reshape(NQ, P).T
    prm[:, Q_NW:Q_NW + NQ] = a["attn_norm_w"].reshape(NQ, P).T
    prm[:, Q_DTB:Q_DTB + NH] = rows(a["attn_dt_bias"])
    prm[:, Q_AL:Q_AL + NH] = rows(a["attn_A_log"])
    bout = np.concatenate([rows(a["ffn_b0b"]), rows(a["ffn_b1b"])], axis=1)

    cst = np.zeros((P, K_END), f)
    cst[:, K_ID:K_ID + 4 * P] = np.tile(np.eye(P, dtype=f), (1, 4))
    cst[:, K_TRI:K_TRI + P] = np.triu(np.ones((P, P), f))
    cst[:, K_SUF:K_SUF + P] = np.tril(np.ones((P, P), f), -1)
    cst[:, K_MASK:K_MASK + DI] = np.kron(np.eye(NH, dtype=f), np.ones((NS, HD), f))
    cst[1:, K_NF] = 1.0

    arrays = {"x": np.ascontiguousarray(a["attn_hidden_states"].reshape(TOKENS, D)), "wa": wa, "wb": wb,
              "win": win, "wout": wout, "prm": prm, "cst": cst, "bout": np.ascontiguousarray(bout)}
    nc = bacc.Bacc("TRN2", target_bir_lowering=False, num_devices=1)
    args = [nc.dram_tensor(f"in_{n}", v.shape, F32, kind="ExternalInput").ap() for n, v in arrays.items()]
    out = nc.dram_tensor("out_0", (TOKENS, D), F32, kind="ExternalOutput").ap()
    macaron(nc, *args, out)
    r = run_bass_kernel_spmd(nc, [{f"in_{n}": v for n, v in arrays.items()}], core_ids=[0])
    return r.results[0]["out_0"].reshape(BATCH, SEQ, D)
```

```python
from contextlib import ExitStack

import concourse.bass as bass
from concourse import mybir

F32 = mybir.dt.float32
F32R = mybir.dt.float32r
ALU = mybir.AluOpType
ACT = mybir.ActivationFunctionType

P = 128
BATCH, SEQ, D = 16, 256, 256
TOKENS = BATCH * SEQ
BLOCK = 512
NBLK = TOKENS // BLOCK
TPB = BLOCK // P
SPB = BLOCK // SEQ
NTILE = TOKENS // P
KD = D // P
FF = 512
NEXP = 2
HT = NEXP * FF // P
DI = 512
NQ = DI // P
NH, HD = 8, 64
NS = 16
TAPS = 4
EPS = 1e-5

W_X, W_G, W_BC, W_DT, W_COLS = 0, DI, 2 * DI, 2 * DI + P, 2 * DI + P + NH
C_ROW = 32

(Q_WG, Q_B0, Q_CW, Q_CB, Q_DS, Q_NW, Q_DTB, Q_AL, Q_END) = (
    0, KD * 2, KD * 2 + HT, KD * 2 + HT + 5 * TAPS, KD * 2 + HT + 5 * TAPS + 5,
    KD * 2 + HT + 5 * TAPS + 5 + NQ, KD * 2 + HT + 5 * TAPS + 5 + 2 * NQ,
    KD * 2 + HT + 5 * TAPS + 5 + 2 * NQ + NH, KD * 2 + HT + 5 * TAPS + 5 + 2 * NQ + 2 * NH)
K_ID, K_TRI, K_SUF, K_MASK, K_NF, K_END = 0, 4 * P, 5 * P, 6 * P, 10 * P, 10 * P + 1

A_LOW, A_HIGH = 60.0, 28.7
FAST = 200.0


def macaron(nc, x, wa, wb, win, wout, params, consts, bout, out):
    ctx = ExitStack()
    with ctx:
        def sb(name, cols, dt=F32):
            return ctx.enter_context(nc.sbuf_tensor(name, [P, cols], dt))

        def sem(name):
            return ctx.enter_context(nc.semaphore(name))

        X = sb("X", NTILE * D)[:, :].rearrange("p (n d) -> p n d", d=D)
        wa_hi = sb("wa_hi", KD * HT * P, F32R)[:, :].rearrange("p (k n) -> p k n", k=KD)
        wa_lo = sb("wa_lo", KD * HT * P, F32R)[:, :].rearrange("p (k n) -> p k n", k=KD)
        wb_hi = sb("wb_hi", HT * D, F32R)[:, :].rearrange("p (k n) -> p k n", k=HT)
        wb_lo = sb("wb_lo", HT * D, F32R)[:, :].rearrange("p (k n) -> p k n", k=HT)
        wi_hi = sb("wi_hi", KD * W_COLS, F32R)[:, :].rearrange("p (k n) -> p k n", k=KD)
        wi_lo = sb("wi_lo", KD * W_COLS, F32R)[:, :].rearrange("p (k n) -> p k n", k=KD)
        wo_hi = sb("wo_hi", NQ * D, F32R)[:, :].rearrange("p (k n) -> p k n", k=NQ)
        wo_lo = sb("wo_lo", NQ * D, F32R)[:, :].rearrange("p (k n) -> p k n", k=NQ)
        wg_hi = sb("wg_hi", KD * 2, F32R)[:, :].rearrange("p (k n) -> p k n", k=KD)
        wg_lo = sb("wg_lo", KD * 2, F32R)[:, :].rearrange("p (k n) -> p k n", k=KD)
        prm = sb("prm", Q_END)
        cst = sb("cst", K_END)
        ident4 = cst[:, K_ID:K_ID + 4 * P]
        ident = cst[:, K_ID:K_ID + P]
        bo = sb("bo", 2 * D)
        xn = sb("xn", TPB * D)[:, :].rearrange("p (n d) -> p n d", d=D)
        xt_hi = sb("xt_hi", KD * BLOCK, F32R)[:, :].rearrange("p (k n) -> p k n", k=KD)
        xt_lo = sb("xt_lo", KD * BLOCK, F32R)[:, :].rearrange("p (k n) -> p k n", k=KD)
        n_wa, n_wb, n_wi, n_wo = KD * HT * P, HT * D, KD * W_COLS, NQ * D
        stage = sb("stage", n_wa + n_wb + n_wi + n_wo)
        st_wa = stage[:, 0:n_wa]
        st_wb = stage[:, n_wa:n_wa + n_wb]
        st_wi = stage[:, n_wa + n_wb:n_wa + n_wb + n_wi]
        st_wo = stage[:, n_wa + n_wb + n_wi:n_wa + n_wb + n_wi + n_wo]
        xs = stage[:, 0:NQ * BLOCK].rearrange("p (q n) -> p q n", q=NQ)
        gs = stage[:, NQ * BLOCK:2 * NQ * BLOCK].rearrange("p (q n) -> p q n", q=NQ)
        xd = stage[:, 2 * NQ * BLOCK:3 * NQ * BLOCK].rearrange("p (q n) -> p q n", q=NQ)
        scratch = sb("scratch", 2 * BLOCK)
        xbuf = sb("xbuf", TPB * D)
        xb = xbuf[:, :].rearrange("p (n d) -> p n d", d=D)
        xdt = [xbuf[:, n * DI:(n + 1) * DI] for n in range(2)]
        st6 = sb("st6", TPB * 6)[:, :].rearrange("p (n d) -> p n d", d=6)
        mv = sb("mv", TPB * 2)[:, :].rearrange("p (n d) -> p n d", d=2)
        mvm = sb("mvm", TPB * 2)[:, :].rearrange("p (n d) -> p n d", d=2)
        mv2 = sb("mv2", NTILE * 2)[:, :].rearrange("p (n d) -> p n d", d=2)
        veps = sb("veps", TPB)
        rstd = sb("rstd", TPB)
        rstd2 = sb("rstd2", NTILE)
        mhalf = sb("mhalf", TPB)
        logit = sb("logit", TPB * 2)[:, :].rearrange("p (n d) -> p n d", d=2)
        sel = sb("sel", TPB)
        m0h = sb("m0h", TPB)
        m1h = sb("m1h", TPB)
        ones = sb("ones", 1)
        dt_raw = sb("dt_raw", NTILE * NH)
        DEC = sb("DEC", 4 * NTILE * NH)
        dec4 = DEC[:, :].rearrange("p (k n) -> p k n", k=4)
        dec = sb("dec", 4 * TPB * NH)
        dec_b = dec[:, :].rearrange("p (k c h) -> p k c h", k=4, c=TPB)
        decay = [sb(f"decay{n}", 4 * P) for n in range(2)]
        M0 = sb("M0", NH * P)
        yg0 = sb("yg0", BLOCK)
        bsel = yg0[:, 0:D]
        sq0 = sb("sq0", BLOCK)
        hid = [scratch[:, 0:BLOCK], scratch[:, BLOCK:2 * BLOCK], sq0[:, :], M0[:, BLOCK:2 * BLOCK]]
        NHID = len(hid)
        scores = sb("scores", BLOCK)
        bt = sb("bt", BLOCK)
        part = bt[:, :].rearrange("p (n d) -> p n d", d=D)
        ct = sb("ct", BLOCK)
        bct = sb("bct", TPB * NS)
        bw = stage[:, (3 * NQ + 2) * BLOCK:(3 * NQ + 2) * BLOCK + SPB * P]
        cp = sb("cp", SPB * P)
        cpt = sb("cpt", SPB * P)
        hst = sb("hst", DI)
        yv = sb("yv", 1)
        yr = sb("yr", 1)
        eA = sb("eA", 4 * NH)
        with nc.sbuf_tensor("hid_hi", [P, HT * BLOCK], F32R) as hh, nc.sbuf_tensor("hid_lo", [P, HT * BLOCK], F32R) as hl:
            hid_hi = hh[:, :].rearrange("p (k n) -> p k n", k=HT)
            hid_lo = hl[:, :].rearrange("p (k n) -> p k n", k=HT)
        gated_hi, gated_lo = sb("gated_hi", 2 * BLOCK, F32R), sb("gated_lo", 2 * BLOCK, F32R)
        y_hi, y_lo = ([g[:, n * BLOCK:(n + 1) * BLOCK] for n in range(2)] for g in (gated_hi, gated_lo))
        xt_last = tuple(g[:, :].rearrange("p (k n) -> p k n", k=KD) for g in (gated_hi, gated_lo))
        M = [M0, sb("M1", NH * P)]
        yg = [yg0, sb("yg1", BLOCK)]
        sq = [sq0, sb("sq1", BLOCK)]
        ssq = [sb(f"ssq{n}", P) for n in range(2)]
        conv_space = sb("conv_space", 6 * BLOCK)
        raw = hid[0:2] + [conv_space[:, n * BLOCK:(n + 1) * BLOCK] for n in range(3)]
        acc = [stage[:, (3 * NQ + n) * BLOCK:(3 * NQ + n + 1) * BLOCK] for n in range(2)] + [
            conv_space[:, n * BLOCK:(n + 1) * BLOCK] for n in range(3, 6)]

        bank = [ctx.enter_context(nc.psum_tensor(f"bank{n}", [P, 512], F32)) for n in range(8)]
        ring, l2p, l1p = bank[0:2], bank[2:4], bank[4:6]
        gatep, dtp = bank[6], bank[7]
        gate_rows, dt_rows = ct[:, :], M0[:, 0:BLOCK]
        decp, pxp, hp, yp, op = bank[2:4], bank[4], bank[5], bank[6], bank[7]

        s_prm, s_cst, s_bo, s_wa, s_wb, s_wi, s_wo, s_out = (
            sem(n) for n in ("params_in", "consts_in", "biases_in", "wa_in", "wb_in", "wi_in", "wo_in", "stored"))
        s_wa = [s_wa, sem("wa_in1")]
        s_x = [sem(f"x_in{n}") for n in range(NBLK)]
        s_id = sem("identity_in")
        w_scaled, w_hi, w_lo = sem("w_scaled"), sem("w_hi"), sem("w_lo")
        s_const, bias_half = sem("const_set"), sem("bias_half")

        def Phase(name, events):
            return {e: sem(f"{name}_{e}") for e in events}

        norm_events = ("bn", "mv", "stats", "rstd", "xn", "xt", "xhi", "xlo")
        ffn_events = norm_events + (
            "gate_rows", "gate_sb", "gate", "gate_read", "picked", "masks", "l1", "act", "hhi", "hlo", "l2", "xb0", "xb",
            "half", "comb", "dt_rows", "dt_sb", "dt", "dt_read", "mvkept")
        fa = Phase("ffn1", ffn_events)
        fb = Phase("ffn2", ffn_events)

        def dve_stats(v, f, s, blk, mvs, wait, wait_rstd):
            wait()
            for t in range(TPB):
                ins = v.bn_stats(st6[:, t, :], X[:, blk * TPB + t, :])
            ins.then_inc(f["bn"], 1)
            v.wait_ge(f["bn"], s + 1)
            if wait_rstd:
                v.wait_ge(f["rstd"], s)
            v.memset(veps[:, :], EPS)
            for t in range(TPB):
                ins = v.bn_aggr(mvs[:, t, :], st6[:, t, :])
            ins.then_inc(f["mv"], 1)
            v.wait_ge(f["mv"], s + 1)
            v.tensor_tensor(veps[:, :], veps[:, :], mvs[:, :, 1], ALU.add).then_inc(f["stats"], 1)

        def pool_rstd(g, f, s, dst):
            g.wait_ge(f["stats"], s + 1)
            g.tensor_tensor(dst, veps[:, :], mhalf[:, :], ALU.pow).then_inc(f["rstd"], 1)

        def dve_apply(v, f, s, blk, mean, rs, first):
            v.wait_ge(f["rstd"], s + 1)
            if not first:
                v.wait_ge(f["xt"], 2 * s)
            for t in range(TPB):
                ins = v.tensor_scalar(xn[:, t, :], X[:, blk * TPB + t, :], mean(t), rs(t),
                                      ALU.subtract, ALU.mult)
            ins.then_inc(f["xn"], 1)

        def pe_turn(pe, f, s, first, banks=ring):
            pe.wait_ge(f["xn"], s + 1)
            for k in range(KD):
                if not first:
                    pe.wait_ge(f["xlo"], 2 * s - 1 + k)
                for t in range(TPB):
                    ins = pe.transpose(banks[k][:, t * P:(t + 1) * P], xn[:, t, k * P:(k + 1) * P], ident)
                ins.then_inc(f["xt"], 1)

        def act_hi(a, f, s, banks=ring, dst=xt_hi):
            for k in range(KD):
                a.wait_ge(f["xt"], 2 * s + k + 1)
                a.activation(dst[:, k, :], banks[k][:, :], ACT.Copy).then_inc(f["xhi"], 1)

        def dve_lo(v, f, s, banks=ring, hi=xt_hi, dst=xt_lo):
            for k in range(KD):
                v.wait_ge(f["xhi"], 2 * s + k + 1)
                v.tensor_tensor(dst[:, k, :], banks[k][:, :], hi[:, k, :].bitcast(F32),
                                ALU.subtract).then_inc(f["xlo"], 1)

        def product(pe, dst, lhs, rhs, ks):
            ks = list(ks)
            for n, k in enumerate(ks):
                pe.matmul(dst, lhs(0, k), rhs(0, k), start=(n == 0), stop=False)
                pe.matmul(dst, lhs(0, k), rhs(1, k), start=False, stop=False)
                ins = pe.matmul(dst, lhs(1, k), rhs(0, k), start=False, stop=(n == len(ks) - 1))
            return ins

        xt = (xt_hi, xt_lo)
        wa2, wb2, wi2, wo2, wg2 = (wa_hi, wa_lo), (wb_hi, wb_lo), (wi_hi, wi_lo), (wo_hi, wo_lo), (wg_hi, wg_lo)
        hid2, y2 = (hid_hi, hid_lo), (y_hi, y_lo)

        def own(dt, i):
            return 2 * i - 1 if dt else i

        def pe_gate(pe, f, i, dt, first):
            s = 0 if first else own(dt, i)
            pe.wait_ge(f["xlo"], 2 * s + 2)
            if not first:
                pe.wait_ge(f["gate_read"], i)
            product(pe, gatep[0:NEXP, :], lambda a, k: wg2[a][:, k, :], lambda a, k: xt[a][:, k, :],
                    range(KD)).then_inc(f["gate_rows"], 1)

        def pe_ffn(pe, f, i, dt, first, last):
            if dt or not first:
                pe_gate(pe, f, i, dt, first)
            for m in range(HT):
                if m == 1:
                    pe_rows_there(pe, f, "gate", i)
                if not (first and m < 2):
                    pe.wait_ge(f["act"], i * HT + m - 1)
                ins = product(pe, l1p[m % 2][:, :], lambda a, k: wa2[a][:, k, m * P:(m + 1) * P],
                              lambda a, k: xt[a][:, k, :], range(KD))
                ins.then_inc(f["l1"], 1)
                if m == 1:
                    pe_columns(pe, f, "gate", i, gatep, gate_rows, NEXP)
            if dt and first:
                pe.wait_ge(w_lo, 4)

            def second(t, e):
                if e == 0 and not (first and t < 2):
                    pe.wait_ge(f["comb"], i * TPB + t - 1)
                return product(pe, l2p[t % 2][:, e * D:(e + 1) * D],
                               lambda a, k: hid2[a][:, k, t * P:(t + 1) * P],
                               lambda a, k: wb2[a][:, k, :], range(4 * e, 4 * e + 4))

            pe.wait_ge(f["hlo"], i * HT + 4)
            second(0, 0)
            second(1, 0)
            if dt and not first:
                pe_turn(pe, f, 2 * i, False)
            if not dt and not last:
                pe_turn(pe, f, own(dt, i + 1), False)
            pe.wait_ge(f["hlo"], i * HT + 8)
            second(0, 1).then_inc(f["l2"], 1)
            if dt and not first:
                pe_dt(pe, f, 2 * i, i - 1)
            if dt and not last:
                pe_turn(pe, f, own(dt, i + 1), False)
            elif dt:
                pe_turn_mix(pe, 0, True)
            if dt and not first:
                pe_rows_there(pe, f, "dt", i - 1)
            second(1, 1).then_inc(f["l2"], 1)
            if dt and not first:
                pe_columns(pe, f, "dt", i - 1, dtp, dt_rows, NH)
            for t in range(2, TPB):
                second(t, 0)
                second(t, 1).then_inc(f["l2"], 1)

        def pe_columns(pe, f, what, b, bank, rows, n):
            for t in range(TPB):
                ins = pe.transpose(bank[:, t * n:(t + 1) * n], rows[0:n, t * P:(t + 1) * P], ident[0:n, 0:n])
            ins.then_inc(f[what], 1)

        def pe_rows_there(pe, f, what, b):
            pe.wait_ge(f[what + "_sb"], b + 1)

        def pe_dt(pe, f, s, b, xt=xt):
            pe.wait_ge(f["xlo"], 2 * s + 2)
            pe.wait_ge(f["dt_read"], b)
            product(pe, dtp[0:NH, :], lambda a, k: wi2[a][:, k, W_DT:W_DT + NH], lambda a, k: xt[a][:, k, :],
                    range(KD)).then_inc(f["dt_rows"], 1)

        def act_rows(a, f, what, b, bank, rows, n):
            a.wait_ge(f[what + "_rows"], b + 1)
            a.activation(rows[0:n, :], bank[0:n, :], ACT.Copy).then_inc(f[what + "_sb"], 1)

        def act_ffn(a, f, i, dt, first, last):
            act_rows(a, f, "gate", i, gatep, gate_rows, NEXP)
            for m in range(HT + 1):
                if m < HT:
                    n = i * HT + m
                    a.wait_ge(f["l1"], n + 1)
                    if not (first and m < NHID):
                        a.wait_ge(f["hlo"], n - NHID + 1)
                    func = ACT.Gelu if m < HT // NEXP else ACT.Relu
                    a.activation(hid[m % NHID], l1p[m % 2][:, :], func,
                                 bias=prm[:, Q_B0 + m:Q_B0 + m + 1]).then_inc(f["act"], 1)
                if m:
                    a.wait_ge(f["act"], i * HT + m)
                    a.activation(hid_hi[:, m - 1, :], hid[(m - 1) % NHID], ACT.Copy).then_inc(f["hhi"], 1)
            if dt and not first:
                act_hi(a, f, 2 * i)
                act_rows(a, f, "dt", i - 1, dtp, dt_rows, NH)
            if not last:
                act_hi(a, f, own(dt, i + 1))

        def dve_ffn(v, f, i, dt, first, last):
            if dt and not first:
                dve_stats_mixer(v, f, i)
            v.wait_ge(f["gate"], i + 1)
            v.tensor_copy(logit, gatep[:, 0:2 * TPB].rearrange("p (n d) -> p n d", d=2)).then_inc(f["gate_read"], 1)
            v.wait_ge(f["gate_read"], i + 1)
            v.tensor_tensor(sel[:, :], logit[:, :, 0], logit[:, :, 1], ALU.is_ge).then_inc(f["picked"], 1)
            v.wait_ge(f["picked"], i + 1)
            if not first:
                v.wait_ge(f["xb"], i * TPB)
            v.tensor_scalar(m0h[:, :], sel[:, :], 0.5, None, ALU.mult)
            v.tensor_scalar(m1h[:, :], sel[:, :], -0.5, 0.5, ALU.mult, ALU.add).then_inc(f["masks"], 1)

            def lo(m):
                v.wait_ge(f["hhi"], i * HT + m + 1)
                v.tensor_tensor(hid_lo[:, m, :], hid[m % NHID], hid_hi[:, m, :].bitcast(F32),
                                ALU.subtract).then_inc(f["hlo"], 1)

            def combine(t):
                n = i * TPB + t
                v.wait_ge(f["l2"], n + 1)
                v.wait_ge(f["xb"], n + 1)
                v.scalar_tensor_tensor(out=part[:, t % 2, :], in0=l2p[t % 2][:, 0:D], scalar=m0h[:, t:t + 1],
                                       in1=xb[:, t, :], op0=ALU.mult, op1=ALU.add).then_inc(f["half"], 1)
                v.wait_ge(f["half"], n + 1)
                v.scalar_tensor_tensor(out=X[:, i * TPB + t, :], in0=l2p[t % 2][:, D:2 * D], scalar=m1h[:, t:t + 1],
                                       in1=part[:, t % 2, :], op0=ALU.mult, op1=ALU.add).then_inc(f["comb"], 1)

            if not last:
                dve_stats_own(v, f, own(dt, i + 1), i + 1)
            for m in range(0, 2):
                lo(m)
            for m in range(2, 4):
                lo(m)
            if dt and not first:
                dve_apply_mixer(v, f, 2 * i, i - 1)
            for m in range(4, 6):
                lo(m)
            if not dt and not last:
                dve_apply_own(v, f, own(dt, i + 1), i + 1)
            for m in range(6, 8):
                lo(m)
            if dt and not first:
                dve_lo(v, f, 2 * i)
            if dt and not last:
                dve_apply_own(v, f, own(dt, i + 1), i + 1)
            elif dt:
                v.wait_ge(f["xt"], 4 * i + 2)
                dve_mix_xn(v, 0, True)
            combine(0)
            if not last:
                dve_lo(v, f, own(dt, i + 1))
            elif dt:
                dve_xt_lo(v, 0)
            for t in range(1, TPB):
                combine(t)
                if dt and not first and t == 1:
                    dve_dt_read(v, f, i - 1)

        def dve_stats_own(v, f, s, blk, first=False):
            def there():
                if f is fa:
                    if isinstance(blk, int):
                        v.wait_ge(s_x[blk], 16)
                    else:
                        for n in range(NBLK):
                            v.wait_ge(s_x[n], 16)
                else:
                    v.wait_ge(mx["fin"], (blk + 1) * TPB if isinstance(blk, int) else NTILE)
            dve_stats(v, f, s, blk, mv, there, not first)

        def dve_apply_own(v, f, s, blk, first=False):
            dve_apply(v, f, s, blk, lambda t: mv[:, t, 0:1], lambda t: rstd[:, t:t + 1], first)

        def dve_stats_mixer(v, f, i, s=None):
            b = i - 1
            dve_stats(v, f, 2 * i if s is None else s, b, mvm,
                      lambda: v.wait_ge(f["comb"], i * TPB), True)
            v.tensor_copy(mv2[:, bass.ds(b * TPB, TPB), :], mvm[:, :, :]).then_inc(f["mvkept"], 1)

        def dve_apply_mixer(v, f, s, b, first=False):
            v.wait_ge(f["mvkept"], b + 1)
            dve_apply(v, f, s, b, lambda t: mv2[:, b * TPB + t, 0:1],
                      lambda t: rstd2[:, bass.ds(b * TPB + t, 1)], first)

        def dve_dt_read(v, f, b):
            v.wait_ge(f["dt"], b + 1)
            v.tensor_copy(dt_raw[:, bass.ds(b * TPB * NH, TPB * NH)], dtp[:, 0:TPB * NH]).then_inc(f["dt_read"], 1)

        def pool_ffn(g, f, i, dt, first, last):
            if dt and not first:
                pool_rstd(g, f, 2 * i, rstd2[:, bass.ds((i - 1) * TPB, TPB)])
            if not last:
                pool_rstd(g, f, own(dt, i + 1), rstd[:, :])
            g.wait_ge(f["masks"], i + 1)
            for t in range(TPB):
                n = i * TPB + t
                if not first:
                    g.wait_ge(f["comb"], n - TPB + 1)
                if not (first and t == 0):
                    g.wait_ge(f["xb"], n)
                g.tensor_tensor(xb[:, t, :], X[:, i * TPB + t, :], bo[:, D:2 * D], ALU.add)
                g.tensor_scalar(bsel, bo[:, 0:D], m0h[:, t:t + 1], None, ALU.mult).then_inc(f["xb0"], 1)
                g.wait_ge(f["xb0"], n + 1)
                g.tensor_tensor(xb[:, t, :], xb[:, t, :], bsel, ALU.add).then_inc(f["xb"], 1)

        def blocks(eng, step):
            step(0, True, False)
            with eng.Fori(1, NBLK - 1) as i:
                step(i, False, False)
            step(NBLK - 1, False, True)

        mx = Phase("mix", ("xn", "xhi",
            "full0", "full1", "free0", "free1", "dec", "tap", "silu", "bcsilu", "xd", "bwcp", "px", "xdt", "decp",
            "scan", "mm0", "mm1", "hp", "hst", "yp", "ysum", "yg", "sq", "ssq0", "ssq", "yhi", "ylo", "op", "yv", "yr",
            "fin"))
        full, free, mm = (mx["full0"], mx["full1"]), (mx["free0"], mx["free1"]), (mx["mm0"], mx["mm1"])
        SLOTS = ["T0", "T1", "BC", "x0", "x1", "x2", "x3", "S", "BCT", "g0", "g1", "CPT", "g2", "g3"]
        CONVS = ["BC", "x0", "x1", "x2", "x3"]
        PER = len(SLOTS) // 2

        def slot(i, what):
            j = SLOTS.index(what)
            return j % 2, i * PER + j // 2

        def fill(pe, sl, first=False):
            b, n = sl
            if not first:
                pe.wait_ge(free[b], n)
            return ring[b], full[b]

        def filled(eng, sl):
            b, n = sl
            eng.wait_ge(full[b], n + 1)
            return ring[b], free[b]

        def emptied(eng, sl):
            b, n = sl
            eng.wait_ge(free[b], n + 1)

        def pe_inproj(pe, sl, col, first=False):
            dst, done = fill(pe, sl, first)
            product(pe, dst[:, :], lambda a, k: wi2[a][:, k, col:col + P],
                    lambda a, k: xt[a][:, k, :], range(KD)).then_inc(done, 1)

        def pe_turn_mix(pe, i, first):
            pe.wait_ge(mx["xn"], i + 1)
            for k in range(KD):
                dst, done = fill(pe, slot(i, f"T{k}"), first)
                for t in range(TPB):
                    ins = pe.transpose(dst[:, t * P:(t + 1) * P], xn[:, t, k * P:(k + 1) * P], ident)
                ins.then_inc(done, 1)

        def pe_conv_in(pe, i, n):
            if n == 0:
                for k in range(KD):
                    emptied(pe, slot(i, f"T{k}"))
            pe_inproj(pe, slot(i, CONVS[n]), W_X + (n - 1) * P if n else W_BC)

        def pe_decay(pe, i, c, first):
            for half in range(2):
                if c == 0 and half == 0:
                    pe.wait_ge(mx["dec"], i + 1)
                if not (first and c == 0):
                    pe.wait_ge(mx["scan"], (i * TPB + c) * 2 + half - 1)
                for h in range(4):
                    ins = pe.transpose(decp[half][:, h * P:(h + 1) * P],
                                       dec_b[:, 0, c, 4 * half + h:4 * half + h + 1].broadcast_to([P, P]), ident)
                ins.then_inc(mx["decp"], 1)

        def pe_px(pe, i, c, first):
            if c == 0:
                pe.wait_ge(mx["silu"], (i + 1) * NQ)
            if not (first and c == 0):
                pe.wait_ge(mx["xdt"], i * TPB + c)
            for q in range(NQ):
                ins = pe.transpose(pxp[:, q * P:(q + 1) * P], xs[:, q, c * P:(c + 1) * P], ident)
            ins.then_inc(mx["px"], 1)

        def pe_state(pe, i, s, first):
            c = 2 * s
            pe.wait_ge(mx["xdt"], i * TPB + c + 1)
            if s == 0:
                pe.wait_ge(mx["bwcp"], i + 1)
            if not (first and s == 0):
                pe.wait_ge(mx["hst"], i * SPB + s)
            pe.matmul(hp[:, :], bw[:, s * P:(s + 1) * P], xdt[c % 2], start=True, stop=True).then_inc(mx["hp"], 1)

        def pe_y(pe, i, c, first):
            n = i * TPB + c
            pe.wait_ge(mx["xdt"], n + 1)
            for half in range(2):
                pe.wait_ge(mm[half], n + 1)
            if not (first and c == 0):
                pe.wait_ge(mx["ysum"], n)
            if c % 2:
                pe.wait_ge(mx["hst"], i * SPB + c // 2 + 1)
                emptied(pe, slot(i, "CPT"))
            for q in range(NQ):
                if c % 2:
                    pe.matmul(yp[:, q * P:(q + 1) * P], hst[:, q * P:(q + 1) * P],
                              cpt[:, (c // 2) * P:(c // 2 + 1) * P], start=True, stop=False, skip_group_check=True)
                for h in range(2):
                    ins = pe.matmul(yp[h * HD:(h + 1) * HD, q * P:(q + 1) * P],
                                    xdt[c % 2][:, (2 * q + h) * HD:(2 * q + h + 1) * HD],
                                    M[c % 2][:, (2 * q + h) * P:(2 * q + h + 1) * P],
                                    start=(c % 2 == 0), stop=True, skip_group_check=True)
            ins.then_inc(mx["yp"], 1)

        def pe_out(pe, n, b, first=False):
            if not first:
                pe.wait_ge(mx["fin"], n)
            pe.wait_ge(mx["ssq"], n + 1)
            pe.matmul(op[:, D:D + 1], ssq[b][:, :], ones[:, :], start=True, stop=True)
            pe.wait_ge(mx["ylo"], n + 1)
            product(pe, op[:, 0:D], lambda a, k: y2[a][b][:, k * P:(k + 1) * P],
                    lambda a, k: wo2[a][:, k, :], range(NQ)).then_inc(mx["op"], 1)

        def pe_bc(pe, i):
            dst, done = fill(pe, slot(i, "S"))
            dst_t, done_t = fill(pe, slot(i, "BCT"))
            pe.wait_ge(mx["bcsilu"], i + 1)
            for c in range(TPB):
                ins = pe.matmul(dst[:, c * P:(c + 1) * P], bt[0:NS, c * P:(c + 1) * P], ct[0:NS, c * P:(c + 1) * P],
                                start=True, stop=True)
            ins.then_inc(done, 1)
            for c in range(TPB):
                src = ct if c % 2 else bt
                ins = pe.transpose(dst_t[:, c * NS:(c + 1) * NS], src[0:NS, c * P:(c + 1) * P], ident[0:NS, 0:NS])
            ins.then_inc(done_t, 1)

        def pe_mix(pe, i, first, last):
            n0 = i * TPB
            if first:
                pe_bc(pe, i)
                for q in range(2):
                    pe_inproj(pe, slot(i, f"g{q}"), W_G + q * P)
                pe_px(pe, i, 0, first)
                pe_tail(pe)
                pe_decay(pe, i, 0, first)
            else:
                pe_inproj(pe, slot(i, "g0"), W_G)
                pe_px(pe, i, 0, first)
                pe_inproj(pe, slot(i, "g1"), W_G + P)
            dst, done = fill(pe, slot(i, "CPT"))
            pe.wait_ge(mx["bwcp"], i + 1)
            for s in range(SPB):
                ins = pe.transpose(dst[:, s * P:(s + 1) * P], cp[:, s * P:(s + 1) * P], ident)
            ins.then_inc(done, 1)
            for c in range(TPB):
                if c + 1 < TPB:
                    pe_px(pe, i, c + 1, first)
                    pe_decay(pe, i, c + 1, first)
                if c % 2 == 0:
                    pe_state(pe, i, c // 2, first)
                if c == 0:
                    for q in range(2, NQ):
                        pe_inproj(pe, slot(i, f"g{q}"), W_G + q * P)
                    if not last:
                        pe_turn_mix(pe, i + 1, False)
                elif c < 3 and not last:
                    pe_conv_in(pe, i + 1, 2 * c - 1)
                pe_y(pe, i, c, first)
                if not (first and c == 0):
                    pe_out(pe, n0 + c - 1, (c - 1) % 2, first and c == 1)
                if 0 < c < 3 and not last:
                    pe_conv_in(pe, i + 1, 2 * c)
                if c == 3 and not last:
                    pe_bc(pe, i + 1)
                    pe_decay(pe, i + 1, 0, False)
                if c == 0 and not last:
                    pe_conv_in(pe, i + 1, 0)
                if c == 1 and last:
                    emptied(pe, slot(i, "g2"))
                    emptied(pe, slot(i, "g3"))
                    pe_turn(pe, fb, 0, True)
            if last:
                pe.wait_ge(mx["ysum"], NTILE)
                pe_gate(pe, fb, 0, False, True)
                pe_out(pe, n0 + TPB - 1, 1)

        def conv_rows(n):
            return slice(0, C_ROW + NS) if n == 0 else slice(0, P)

        def tap_count(i, n, back):
            return i * 5 * 3 + (n // 2 * 6 + (back - 1) * 2 + n % 2 + 1 if n < 4 else 12 + back)

        def act_raw(a, i, n, first):
            src, done = filled(a, slot(i, CONVS[n]))
            r = conv_rows(n)
            if not first:
                if n == 0:
                    a.wait_ge(mx["bcsilu"], i)
                else:
                    a.wait_ge(mx["silu"], (i - 1) * NQ + n)
            cw = Q_CW + n * TAPS
            a.activation(raw[n][r, :], src[r, :], ACT.Copy)
            a.activation(acc[n][r, :], src[r, :], ACT.Identity, bias=prm[r, Q_CB + n:Q_CB + n + 1],
                         scale=prm[r, cw + 3:cw + 4]).then_inc(done, 1)

        def dve_tap(v, i, n, back):
            if back == 1:
                emptied(v, slot(i, CONVS[n]))
            else:
                v.wait_ge(mx["tap"], tap_count(i, n, back - 1))
            r = conv_rows(n)
            rows = raw[n][r, :].rearrange("p (s t) -> p s t", s=SPB)
            accs = acc[n][r, :].rearrange("p (s t) -> p s t", s=SPB)
            w = Q_CW + n * TAPS + 3 - back
            v.scalar_tensor_tensor(out=accs[:, :, back:], in0=rows[:, :, 0:SEQ - back], scalar=prm[r, w:w + 1],
                                   in1=accs[:, :, back:], op0=ALU.mult, op1=ALU.add).then_inc(mx["tap"], 1)

        def act_silu_bc(a, i, first):
            a.wait_ge(mx["tap"], tap_count(i, 0, 3))
            if not first:
                b, n = slot(i - 1, "BCT")
                a.wait_ge(full[b], n + 1)
            a.activation(bt[0:NS, :], acc[0][0:NS, :], ACT.Silu)
            a.activation(ct[0:NS, :], acc[0][C_ROW:C_ROW + NS, :], ACT.Silu).then_inc(mx["bcsilu"], 1)

        def act_silu_x(a, i, q, first):
            a.wait_ge(mx["tap"], tap_count(i, 1 + q, 3))
            if not first:
                if q == 0:
                    a.wait_ge(mx["px"], i * TPB)
                a.wait_ge(mx["xd"], (i - 1) * NQ + q + 1)
            a.activation(xs[:, q, :], acc[1 + q], ACT.Silu).then_inc(mx["silu"], 1)

        def act_xd(a, i, q, first):
            if not first and q == 0:
                a.wait_ge(mx["ysum"], i * TPB)
            a.wait_ge(mx["silu"], i * NQ + q + 1)
            a.activation(xd[:, q, :], xs[:, q, :], ACT.Copy, scale=prm[:, Q_DS + q:Q_DS + q + 1]).then_inc(mx["xd"], 1)

        def act_gate(a, i, q, first):
            src, done = filled(a, slot(i, f"g{q}"))
            if not first and q == 0:
                a.wait_ge(mx["yg"], i * TPB)
            a.activation(gs[:, q, :], src[:, :], ACT.Silu).then_inc(done, 1)

        def act_copy(a, i, what, dst, cols, wait):
            src, done = filled(a, slot(i, what))
            wait()
            a.activation(dst, src[:, 0:cols], ACT.Copy).then_inc(done, 1)

        def act_out(a, i, c, first):
            n = i * TPB + c
            if not (first and c < 2):
                a.wait_ge(mx["ssq"], n - 1)
            a.wait_ge(mx["yg"], n + 1)
            a.activation(sq[c % 2][:, :], yg[c % 2][:, :], ACT.Square).then_inc(mx["sq"], 1)
            if not (first and c < 2):
                a.wait_ge(mx["op"], n - 1)
            a.activation(y_hi[c % 2], yg[c % 2][:, :], ACT.Copy).then_inc(mx["yhi"], 1)

        def act_xt_hi(a, i, first):
            for k in range(KD):
                src, _ = filled(a, slot(i, f"T{k}"))
                if k == 0 and not first:
                    b, n = slot(i - 1, "g3")
                    a.wait_ge(full[b], n + 1)
                a.activation(xt_hi[:, k, :], src[:, :], ACT.Copy).then_inc(mx["xhi"], 1)

        def dve_xt_lo(v, i):
            for k in range(KD):
                v.wait_ge(mx["xhi"], 2 * i + k + 1)
                b, _ = slot(i, f"T{k}")
                v.tensor_tensor(xt_lo[:, k, :], ring[b][:, :], xt_hi[:, k, :].bitcast(F32),
                                ALU.subtract).then_inc(free[b], 1)

        def act_ahead(a, i, c, first):
            if c == 0:
                act_xt_hi(a, i, first)
                act_raw(a, i, 0, first)
            elif c < 3:
                act_raw(a, i, 2 * c, first)
                if c == 2:
                    act_silu_bc(a, i, first)
            else:
                for q in range(NQ - 1):
                    act_silu_x(a, i, q, first)

        def act_bc(a, i, first):
            def scores_free():
                if not first:
                    for half in range(2):
                        a.wait_ge(mm[half], i * TPB)
            act_copy(a, i, "S", scores[:, :], BLOCK, scores_free)

            def bct_free():
                if not first:
                    a.wait_ge(mx["bwcp"], i)
            act_copy(a, i, "BCT", bct[:, :], TPB * NS, bct_free)

        def act_mix(a, i, first, last):
            if first:
                act_bc(a, i, first)
            act_silu_x(a, i, NQ - 1, first)
            if first:
                act_tail(a)
                a.wait_ge(tail["done"], 1)
            act_gate(a, i, 0, first)
            act_gate(a, i, 1, first)

            def cpt_free():
                if not first:
                    a.wait_ge(mx["yp"], i * TPB)
            act_copy(a, i, "CPT", cpt[:, :], SPB * P, cpt_free)
            for q in range(NQ):
                act_xd(a, i, q, first)
            act_gate(a, i, 2, first)
            act_gate(a, i, 3, first)
            for c in range(TPB):
                if c == 0 and not last:
                    act_ahead(a, i + 1, c, False)
                elif c < 3 and not last:
                    act_raw(a, i + 1, 2 * c - 1, False)
                elif not last:
                    act_ahead(a, i + 1, c, False)
                act_out(a, i, c, first)
                if c == 3 and not last:
                    act_bc(a, i + 1, False)
                if 0 < c < 3 and not last:
                    act_ahead(a, i + 1, c, False)
                if c == 1 and last:
                    act_hi(a, fb, 0)

        def dve_scan_half(v, i, c, half, first):
            n = (i * TPB + c) * 2 + half
            v.wait_ge(mx["decp"], n + 1)
            if not (first and c == 0):
                v.wait_ge(mm[half], i * TPB + c)
            v.tensor_tensor_scan(decay[half][:, :], decp[half][:, :], ident4, 0.0,
                                 ALU.mult, ALU.add).then_inc(mx["scan"], 1)

        DVE_HALVES = ((0, 1), (0,), (0,), ())
        POOL_HALVES = ((), (1,), (1,), (0, 1))

        def matrix(eng, i, c, half, first):
            n = i * TPB + c
            if c == 0:
                emptied(eng, slot(i, "S"))
            if not (first and c < 2):
                eng.wait_ge(mx["yp"], n - 1)
            eng.wait_ge(mx["scan"], 2 * n + half + 1)
            eng.tensor_tensor(M[c % 2][:, half * 4 * P:(half + 1) * 4 * P].rearrange("p (h t) -> p h t", h=4),
                              decay[half][:, :].rearrange("p (h t) -> p h t", h=4),
                              scores[:, c * P:(c + 1) * P].unsqueeze(1).broadcast_to([P, 4, P]),
                              ALU.mult).then_inc(mm[half], 1)

        def dve_xdt(v, i, c, first):
            n = i * TPB + c
            v.wait_ge(mx["px"], n + 1)
            if not (first and c < 2):
                v.wait_ge(mx["yp"], n - 1)
            v.tensor_tensor(xdt[c % 2].rearrange("p (h d) -> p h d", h=NH),
                            pxp[:, :].rearrange("p (h d) -> p h d", h=NH),
                            dec_b[:, 1, c, :].unsqueeze(2).broadcast_to([P, NH, HD]), ALU.mult).then_inc(mx["xdt"], 1)

        def dve_scaled_bc(v, i, first):
            emptied(v, slot(i, "BCT"))
            if not first:
                v.wait_ge(mx["hp"], i * SPB)
            for s in range(SPB):
                for dst, c, kind in ((bw, 2 * s, 3), (cp, 2 * s + 1, 2)):
                    ins = v.tensor_tensor(dst[:, s * P:(s + 1) * P].rearrange("p (h n) -> p h n", h=NH),
                                          bct[:, c * NS:(c + 1) * NS].unsqueeze(1).broadcast_to([P, NH, NS]),
                                          dec_b[:, kind, c, :].unsqueeze(2).broadcast_to([P, NH, NS]), ALU.mult)
            ins.then_inc(mx["bwcp"], 1)

        def dve_state(v, i, s, first):
            v.wait_ge(mx["hp"], i * SPB + s + 1)
            if not (first and s == 0):
                v.wait_ge(mx["yp"], i * TPB + 2 * s)
            v.tensor_tensor(hst[:, :], hp[:, :], cst[:, K_MASK:K_MASK + DI], ALU.mult).then_inc(mx["hst"], 1)

        def dve_y(v, i, c, first):
            n = i * TPB + c
            if c == 0:
                v.wait_ge(mx["xd"], (i + 1) * NQ)
            if not (first and c < 2):
                v.wait_ge(mx["sq"], n - 1)
                v.wait_ge(mx["yhi"], n - 1)
                v.wait_ge(mx["ylo"], n - 1)
            v.wait_ge(mx["yp"], n + 1)
            here = slice(c * P, (c + 1) * P)
            y4 = yg[c % 2][:, :].rearrange("p (q t) -> p q t", q=NQ)
            v.tensor_tensor(y4, yp[:, :].rearrange("p (q t) -> p q t", q=NQ), xd[:, :, here],
                            ALU.add).then_inc(mx["ysum"], 1)
            v.wait_ge(mx["ysum"], n + 1)
            if c == 0:
                emptied(v, slot(i, "g3"))
            v.tensor_tensor(y4, y4, gs[:, :, here], ALU.mult).then_inc(mx["yg"], 1)

        def dve_mean_square(v, n, first=False):
            if not first:
                v.wait_ge(mx["yr"], n)
            v.wait_ge(mx["op"], n + 1)
            v.tensor_scalar(yv[:, :], op[:, D:D + 1], 1.0 / DI, EPS, ALU.mult, ALU.add).then_inc(mx["yv"], 1)

        def dve_final(v, n):
            v.wait_ge(mx["yr"], n + 1)
            v.scalar_tensor_tensor(out=X[:, n, :], in0=op[:, 0:D], scalar=yr[:, :], in1=X[:, n, :],
                                   op0=ALU.mult, op1=ALU.add).then_inc(mx["fin"], 1)

        def pool_rms(g, n, first=False):
            if not first:
                g.wait_ge(mx["fin"], n)
            g.wait_ge(mx["yv"], n + 1)
            g.tensor_tensor(yr[:, :], yv[:, :], mhalf[:, 0:1], ALU.pow).then_inc(mx["yr"], 1)

        def pool_out(g, i, c, first):
            n, b = i * TPB + c, c % 2
            g.wait_ge(mx["sq"], n + 1)
            g.tensor_tensor(sq[b][:, 0:2 * P], sq[b][:, 0:2 * P], sq[b][:, 2 * P:4 * P], ALU.add).then_inc(mx["ssq0"], 1)
            if c:
                pool_rms(g, n - 1, first and c == 1)
            if not (first and c < 2):
                g.wait_ge(mx["op"], n - 1)
            g.wait_ge(mx["yhi"], n + 1)
            g.tensor_tensor(y_lo[b], yg[b][:, :], y_hi[b].bitcast(F32), ALU.subtract).then_inc(mx["ylo"], 1)
            g.wait_ge(mx["ssq0"], n + 1)
            g.tensor_tensor(ssq[b][:, :], sq[b][:, 0:P], sq[b][:, P:2 * P], ALU.add).then_inc(mx["ssq"], 1)

        def pool_mix(g, i, first, last):
            n0 = i * TPB
            if last:
                pool_rstd(g, fb, 0, rstd[:, :])
            for c in range(TPB):
                if c + 1 < TPB:
                    for half in POOL_HALVES[c + 1]:
                        matrix(g, i, c + 1, half, first)
                if c == 0 and not first:
                    pool_rms(g, n0 - 1)
                pool_out(g, i, c, first)
            if last:
                pool_rms(g, n0 + 3)

        def dve_dec(v, i, first):
            if not first:
                v.wait_ge(mx["bwcp"], i)
                v.wait_ge(mx["decp"], i * TPB * 2)
            v.tensor_copy(dec[:, :].rearrange("p (k n) -> p k n", k=4),
                          dec4[:, :, bass.ds(i * TPB * NH, TPB * NH)]).then_inc(mx["dec"], 1)
            v.wait_ge(mx["dec"], i + 1)

        def dve_mix_xn(v, i, first):
            if not first:
                filled(v, slot(i - 1, "T1"))
            for t in range(TPB):
                ins = v.tensor_scalar(xn[:, t, :], X[:, i * TPB + t, :], mv2[:, i * TPB + t, 0:1],
                                      rstd2[:, bass.ds(i * TPB + t, 1)], ALU.subtract, ALU.mult)
            ins.then_inc(mx["xn"], 1)

        def dve_mix(v, i, first, last):
            n0 = i * TPB
            if first:
                dve_dec(v, i, first)
            dve_scan_half(v, i, 0, 0, first)
            dve_scan_half(v, i, 0, 1, first)
            if not first:
                dve_final(v, n0 - 2)
            dve_scaled_bc(v, i, first)
            dve_xdt(v, i, 0, first)
            for half in DVE_HALVES[0]:
                matrix(v, i, 0, half, first)
            if not last:
                dve_mix_xn(v, i + 1, False)
            else:
                dve_stats_own(v, fb, 0, 0, True)
            for c in range(TPB):
                if c + 1 < TPB:
                    dve_xdt(v, i, c + 1, first)
                    dve_scan_half(v, i, c + 1, 0, first)
                    dve_scan_half(v, i, c + 1, 1, first)
                if c == 1 and not first:
                    dve_final(v, n0 - 1)
                if c % 2 == 0:
                    dve_state(v, i, c // 2, first)
                if c + 1 < TPB:
                    for half in DVE_HALVES[c + 1]:
                        matrix(v, i, c + 1, half, first)
                if c == 0 and not last:
                    dve_xt_lo(v, i + 1)
                if c == 3 and not last:
                    dve_dec(v, i + 1, False)
                dve_y(v, i, c, first)
                if c == 0 and not first:
                    dve_mean_square(v, n0 - 1)
                if c:
                    tiles = ((0, 1), (2, 3), (4,))[c - 1]
                    for back in range(1, TAPS):
                        if not last:
                            for tile in tiles:
                                dve_tap(v, i + 1, tile, back)
                        if back == (1 if c < 3 else 3):
                            dve_mean_square(v, n0 + c - 1, first and c == 1)
                        elif back == 2 and c < 3:
                            dve_final(v, n0 + c - 1)
                if c == 0 and last:
                    filled(v, slot(i, "T1"))
                    dve_apply_own(v, fb, 0, 0, True)
                if c == 2 and last:
                    dve_lo(v, fb, 0)
            if last:
                dve_final(v, n0 + 2)
                dve_mean_square(v, n0 + 3)
                dve_final(v, n0 + 3)

        tail = Phase("dt", ("v", "av", "e", "u", "ln", "um1", "z", "rec", "q", "q2", "ez", "dt0", "dt",
                            "clip", "eA", "a1", "a2", "a", "dA", "cum", "P", "done"))
        NA = NTILE * NH
        tmp = [stage[:, 2 * NQ * BLOCK + n * NA:2 * NQ * BLOCK + (n + 1) * NA] for n in range(8)]
        t_v, t_a, t_e, t_u, t_l, t_z, t_r, t_q = tmp
        dt_all, dA_all = dec4[:, 1, :], dec4[:, 0, :]

        def per_head(col):
            return eA[:, col * NH:(col + 1) * NH].unsqueeze(1).broadcast_to([P, NTILE, NH])

        def by_head(ap):
            return ap.rearrange("p (n h) -> p n h", h=NH)

        def dve_tail(v):
            def step(ins, s):
                ins.then_inc(s, 1)
                v.wait_ge(s, 1)

            v.wait_ge(fa["dt_read"], NBLK)
            step(v.tensor_tensor(by_head(t_v), by_head(dt_raw[:, :]),
                                 prm[:, Q_DTB:Q_DTB + NH].unsqueeze(1).broadcast_to([P, NTILE, NH]), ALU.add), tail["v"])
            step(v.scalar_tensor_tensor(out=t_a, in0=t_v, scalar=-1.0, in1=t_v, op0=ALU.mult, op1=ALU.max), tail["av"])
            v.tensor_scalar(eA[:, 0:NH], prm[:, Q_AL:Q_AL + NH], A_LOW, None, ALU.min)
            step(v.tensor_scalar(eA[:, NH:2 * NH], prm[:, Q_AL:Q_AL + NH], A_LOW, 0.0, ALU.subtract, ALU.max), tail["clip"])
            v.tensor_scalar(eA[:, NH:2 * NH], eA[:, NH:2 * NH], A_HIGH, None, ALU.min).then_inc(tail["clip"], 1)
            v.wait_ge(tail["e"], 1)
            step(v.tensor_scalar(t_u, t_e, 1.0, None, ALU.add), tail["u"])
            step(v.tensor_scalar(t_z, t_u, 1.0, None, ALU.is_equal), tail["z"])
            step(v.scalar_tensor_tensor(out=t_r, in0=t_u, scalar=1.0, in1=t_z, op0=ALU.subtract, op1=ALU.add), tail["um1"])
            step(v.reciprocal(t_r, t_r), tail["rec"])
            v.tensor_tensor(t_z, t_z, t_e, ALU.mult).then_inc(tail["ez"], 1)
            v.wait_ge(tail["ln"], 1)
            step(v.tensor_tensor(t_q, t_l, t_e, ALU.mult), tail["q"])
            step(v.tensor_tensor(t_q, t_q, t_r, ALU.mult), tail["q2"])
            v.wait_ge(tail["ez"], 1)
            step(v.tensor_tensor(t_q, t_q, t_z, ALU.add), tail["dt0"])
            step(v.scalar_tensor_tensor(out=dt_all, in0=t_v, scalar=0.0, in1=t_q, op0=ALU.max, op1=ALU.add), tail["dt"])
            v.wait_ge(tail["eA"], 1)
            step(v.tensor_tensor(by_head(t_a), by_head(dt_all), per_head(2), ALU.mult), tail["a1"])
            step(v.scalar_tensor_tensor(out=by_head(t_a), in0=by_head(t_a), scalar=FAST, in1=per_head(3),
                                        op0=ALU.min, op1=ALU.mult), tail["a2"])
            step(v.tensor_scalar(t_a, t_a, FAST, None, ALU.min), tail["a"])
            v.wait_ge(tail["dA"], 1)
            v.tensor_scalar(dA_all, t_u, cst[:, K_NF:K_NF + 1], None, ALU.mult).then_inc(tail["done"], 1)
            v.wait_ge(tail["P"], 2)
            v.wait_ge(tail["done"], 1)

        def act_tail(a):
            a.wait_ge(tail["av"], 1)
            a.activation(t_e, t_a, ACT.Exp, scale=-1.0).then_inc(tail["e"], 1)
            a.wait_ge(tail["clip"], 2)
            a.activation(eA[:, 2 * NH:4 * NH], eA[:, 0:2 * NH], ACT.Exp).then_inc(tail["eA"], 1)
            a.wait_ge(tail["u"], 1)
            a.activation(t_l, t_u, ACT.Ln).then_inc(tail["ln"], 1)
            a.wait_ge(tail["a"], 1)
            a.wait_ge(tail["um1"], 1)
            a.activation(t_u, t_a, ACT.Exp, scale=-1.0).then_inc(tail["dA"], 1)
            a.wait_ge(tail["cum"], 1)
            a.activation(dec4[:, 2, :], yp[:, 0:NA], ACT.Exp, scale=-1.0).then_inc(tail["P"], 1)
            a.activation(dec4[:, 3, :], yp[:, NA:2 * NA], ACT.Exp, scale=-1.0).then_inc(tail["P"], 1)

        def pe_tail(pe):
            pe.wait_ge(tail["a"], 1)
            pe.matmul(yp[:, 0:NA], cst[:, K_TRI:K_TRI + P], t_a, start=True, stop=True)
            pe.matmul(yp[:, NA:2 * NA], cst[:, K_SUF:K_SUF + P], t_a, start=True, stop=True).then_inc(tail["cum"], 1)

        block = ctx.enter_context(nc.Block())

        @block.sync
        def _(sp):
            xv = x.rearrange("(i t p) d -> i p t d", t=TPB, p=P)
            ov = out.rearrange("(i t p) d -> i p t d", t=TPB, p=P)
            sp.dma_start(X[:, 0:TPB, :], xv[0]).then_inc(s_x[0], 16)
            sp.dma_start(prm[:, :], params).then_inc(s_prm, 16)
            sp.dma_start(cst[:, 0:P], consts[:, 0:P]).then_inc(s_id, 16)
            for k in range(KD):
                half = slice(k * HT * P, (k + 1) * HT * P)
                sp.dma_start(st_wa[:, half], wa[:, half]).then_inc(s_wa[k], 16)
            sp.dma_start(X[:, TPB:2 * TPB, :], xv[1]).then_inc(s_x[1], 16)
            sp.dma_start(st_wb, wb).then_inc(s_wb, 16)
            sp.dma_start(bo[:, :], bout).then_inc(s_bo, 16)
            sp.dma_start(st_wi, win).then_inc(s_wi, 16)
            sp.dma_start(cst[:, P:K_END], consts[:, P:K_END]).then_inc(s_cst, 16)
            sp.dma_start(st_wo, wout).then_inc(s_wo, 16)
            for n in range(2, NBLK):
                sp.dma_start(X[:, n * TPB:(n + 1) * TPB, :], xv[n]).then_inc(s_x[n], 16)
            with sp.Fori(0, NBLK) as i:
                sp.wait_ge(fb["comb"], i * TPB + TPB)
                sp.dma_start(ov[i], X[:, bass.ds(i * TPB, TPB), :]).then_inc(s_out, 16)
            sp.wait_ge(s_out, 16 * NBLK)

        @block.gpsimd
        def _(g):
            g.memset(mhalf[:, :], -0.5).then_inc(s_const, 1)
            g.memset(ones[:, :], 1.0).then_inc(s_const, 1)
            g.wait_ge(s_const, 2)
            pool_rstd(g, fa, 0, rstd[:, :])

            g.wait_ge(s_bo, 16)
            g.tensor_tensor(bo[:, 0:D], bo[:, 0:D], bo[:, D:2 * D], ALU.subtract).then_inc(bias_half, 1)
            g.wait_ge(bias_half, 1)
            g.tensor_scalar(bo[:, D:2 * D], bo[:, D:2 * D], 0.5, None, ALU.mult).then_inc(bias_half, 1)
            g.wait_ge(s_wo, 16)
            g.wait_ge(s_prm, 16)
            for q in range(NQ):
                ins = g.tensor_scalar(st_wo[:, q * D:(q + 1) * D], st_wo[:, q * D:(q + 1) * D],
                                      prm[:, Q_NW + q:Q_NW + q + 1], None, ALU.mult)
            ins.then_inc(w_scaled, 1)
            g.wait_ge(bias_half, 2)
            blocks(g, lambda i, first, last: pool_ffn(g, fa, i, True, first, last))
            pool_rstd(g, fa, 2 * NBLK - 1, rstd2[:, (NBLK - 1) * TPB:NTILE])
            blocks(g, lambda i, first, last: pool_mix(g, i, first, last))
            blocks(g, lambda i, first, last: pool_ffn(g, fb, i, False, first, last))

        @block.scalar
        def _(a):
            a.wait_ge(s_prm, 16)
            a.activation(wg_hi.rearrange("p k n -> p (k n)"), prm[:, Q_WG:Q_WG + KD * 2], ACT.Copy).then_inc(w_hi, 1)
            for k in range(KD):
                a.wait_ge(s_wa[k], 16)
                a.activation(wa_hi[:, k, :], st_wa[:, k * HT * P:(k + 1) * HT * P], ACT.Copy).then_inc(w_hi, 1)
                a.wait_ge(fa["xt"], k + 1)
                a.activation(xt_hi[:, k, :], ring[k][:, :], ACT.Copy).then_inc(fa["xhi"], 1)

            def hi(dst, src):
                a.activation(dst.rearrange("p k n -> p (k n)"), src, ACT.Copy).then_inc(w_hi, 1)

            a.wait_ge(s_wb, 16)
            hi(wb_hi, st_wb)
            a.wait_ge(s_wi, 16)
            hi(wi_hi, st_wi)
            act_ffn(a, fa, 0, True, True, False)
            a.wait_ge(w_scaled, 1)
            hi(wo_hi, st_wo)
            with a.Fori(1, NBLK - 1) as i:
                act_ffn(a, fa, i, True, False, False)
            act_ffn(a, fa, NBLK - 1, True, False, True)
            act_xt_hi(a, 0, True)
            act_raw(a, 0, 0, True)
            act_raw(a, 0, 1, True)
            act_raw(a, 0, 2, True)
            act_raw(a, 0, 3, True)
            act_raw(a, 0, 4, True)
            act_hi(a, fa, 2 * NBLK - 1, l1p, xt_last[0])
            act_rows(a, fa, "dt", NBLK - 1, dtp, dt_rows, NH)
            act_silu_bc(a, 0, True)
            for q in range(NQ - 1):
                act_silu_x(a, 0, q, True)
            blocks(a, lambda i, first, last: act_mix(a, i, first, last))
            blocks(a, lambda i, first, last: act_ffn(a, fb, i, False, first, last))

        @block.vector
        def _(v):
            dve_stats_own(v, fa, 0, 0, True)
            v.wait_ge(s_prm, 16)
            v.wait_ge(w_hi, 1)
            v.tensor_tensor(wg_lo.rearrange("p k n -> p (k n)"), prm[:, Q_WG:Q_WG + KD * 2],
                            wg_hi.rearrange("p k n -> p (k n)").bitcast(F32), ALU.subtract).then_inc(w_lo, 1)
            dve_apply_own(v, fa, 0, 0, True)
            for k in range(KD):
                v.wait_ge(w_hi, k + 2)
                v.tensor_tensor(wa_lo[:, k, :], st_wa[:, k * HT * P:(k + 1) * HT * P], wa_hi[:, k, :].bitcast(F32),
                                ALU.subtract).then_inc(w_lo, 1)
                v.wait_ge(fa["xhi"], k + 1)
                v.tensor_tensor(xt_lo[:, k, :], ring[k][:, :], xt_hi[:, k, :].bitcast(F32),
                                ALU.subtract).then_inc(fa["xlo"], 1)

            def lo(dst, hi, src, n):
                v.wait_ge(w_hi, n)
                v.tensor_tensor(dst.rearrange("p k n -> p (k n)"), src,
                                hi.rearrange("p k n -> p (k n)").bitcast(F32), ALU.subtract).then_inc(w_lo, 1)

            lo(wb_lo, wb_hi, st_wb, 4)
            lo(wi_lo, wi_hi, st_wi, 5)
            dve_ffn(v, fa, 0, True, True, False)
            lo(wo_lo, wo_hi, st_wo, 6)
            with v.Fori(1, NBLK - 1) as i:
                dve_ffn(v, fa, i, True, False, False)
            dve_ffn(v, fa, NBLK - 1, True, False, True)
            dve_stats_mixer(v, fa, NBLK, 2 * NBLK - 1)
            for back in range(1, TAPS):
                dve_tap(v, 0, 0, back)
                dve_tap(v, 0, 1, back)
            filled(v, slot(0, "T1"))
            dve_apply_mixer(v, fa, 2 * NBLK - 1, NBLK - 1)
            dve_tap(v, 0, 2, 1)
            dve_tap(v, 0, 3, 1)
            dve_tap(v, 0, 2, 2)
            dve_lo(v, fa, 2 * NBLK - 1, l1p, *xt_last)
            dve_tap(v, 0, 3, 2)
            dve_tap(v, 0, 2, 3)
            dve_tap(v, 0, 3, 3)
            for back in range(1, TAPS):
                dve_tap(v, 0, 4, back)
            dve_dt_read(v, fa, NBLK - 1)
            dve_tail(v)
            blocks(v, lambda i, first, last: dve_mix(v, i, first, last))
            blocks(v, lambda i, first, last: dve_ffn(v, fb, i, False, first, last))

        @block.tensor
        def _(pe):
            pe.wait_ge(s_id, 16)
            pe_turn(pe, fa, 0, True)
            pe.wait_ge(w_lo, 3)
            pe_ffn(pe, fa, 0, True, True, False)
            pe.wait_ge(w_lo, 5)
            with pe.Fori(1, NBLK - 1) as i:
                pe_ffn(pe, fa, i, True, False, False)
            pe_ffn(pe, fa, NBLK - 1, True, False, True)
            pe.wait_ge(w_lo, 6)
            pe.wait_ge(s_cst, 16)
            pe.wait_ge(s_const, 2)
            for n in range(5):
                pe_conv_in(pe, 0, n)
            pe_turn(pe, fa, 2 * NBLK - 1, False, l1p)
            pe_dt(pe, fa, 2 * NBLK - 1, NBLK - 1, xt_last)
            pe_rows_there(pe, fa, "dt", NBLK - 1)
            pe_columns(pe, fa, "dt", NBLK - 1, dtp, dt_rows, NH)
            blocks(pe, lambda i, first, last: pe_mix(pe, i, first, last))
            pe.wait_ge(mx["fin"], NTILE)
            blocks(pe, lambda i, first, last: pe_ffn(pe, fb, i, False, first, last))


def kernel(**inputs):
    import numpy as np
    import concourse.bacc as bacc
    from concourse.bass_utils import run_bass_kernel_spmd

    a = {n.replace("L0_", ""): np.asarray(v) for n, v in inputs.items()}
    f = np.float32

    def tiles(w, k):
        return np.ascontiguousarray(w.reshape(k, P, -1).transpose(1, 0, 2).reshape(P, -1))

    def rows(v):
        return np.broadcast_to(v.reshape(1, -1), (P, v.size))

    wa = tiles(np.concatenate([a["ffn_W0a"], a["ffn_W1a"]]).T, KD)
    wb = tiles(np.concatenate([a["ffn_W0b"].T, a["ffn_W1b"].T]), HT)
    w = a["attn_W_in"]
    wi = np.zeros((D, W_COLS), f)
    wi[:, W_X:W_X + DI] = w[:, DI:2 * DI]
    wi[:, W_G:W_G + DI] = w[:, 0:DI]
    wi[:, W_BC:W_BC + NS] = w[:, 2 * DI:2 * DI + NS]
    wi[:, W_BC + C_ROW:W_BC + C_ROW + NS] = w[:, 2 * DI + NS:2 * DI + 2 * NS]
    wi[:, W_DT:W_DT + NH] = w[:, 2 * DI + 2 * NS:]
    win = tiles(wi, KD)
    wout = tiles(a["attn_W_out"], NQ)

    prm = np.zeros((P, Q_END), f)
    prm[:, Q_WG:Q_WG + 2 * KD] = tiles(a["ffn_Wg"].T, KD)
    prm[:, Q_B0:Q_B0 + HT] = np.concatenate([a["ffn_b0a"], a["ffn_b1a"]]).reshape(HT, P).T
    cw, cb = a["attn_conv_w"], a["attn_conv_b"]
    for n in range(5):
        for at, lo, hi in ([(0, DI, DI + NS), (C_ROW, DI + NS, DI + 2 * NS)] if n == 0 else
                           [(0, (n - 1) * P, n * P)]):
            prm[at:at + hi - lo, Q_CW + n * TAPS:Q_CW + (n + 1) * TAPS] = cw[lo:hi]
            prm[at:at + hi - lo, Q_CB + n] = cb[lo:hi]
    prm[:, Q_DS:Q_DS + NQ] = np.repeat(a["attn_D_skip"], HD).reshape(NQ, P).T
    prm[:, Q_NW:Q_NW + NQ] = a["attn_norm_w"].reshape(NQ, P).T
    prm[:, Q_DTB:Q_DTB + NH] = rows(a["attn_dt_bias"])
    prm[:, Q_AL:Q_AL + NH] = rows(a["attn_A_log"])
    bout = np.concatenate([rows(a["ffn_b0b"]), rows(a["ffn_b1b"])], axis=1)

    cst = np.zeros((P, K_END), f)
    cst[:, K_ID:K_ID + 4 * P] = np.tile(np.eye(P, dtype=f), (1, 4))
    cst[:, K_TRI:K_TRI + P] = np.triu(np.ones((P, P), f))
    cst[:, K_SUF:K_SUF + P] = np.tril(np.ones((P, P), f), -1)
    cst[:, K_MASK:K_MASK + DI] = np.kron(np.eye(NH, dtype=f), np.ones((NS, HD), f))
    cst[1:, K_NF] = 1.0

    arrays = {"x": np.ascontiguousarray(a["attn_hidden_states"].reshape(TOKENS, D)), "wa": wa, "wb": wb,
              "win": win, "wout": wout, "prm": prm, "cst": cst, "bout": np.ascontiguousarray(bout)}
    nc = bacc.Bacc("TRN2", target_bir_lowering=False, num_devices=1)
    args = [nc.dram_tensor(f"in_{n}", v.shape, F32, kind="ExternalInput").ap() for n, v in arrays.items()]
    out = nc.dram_tensor("out_0", (TOKENS, D), F32, kind="ExternalOutput").ap()
    macaron(nc, *args, out)
    r = run_bass_kernel_spmd(nc, [{f"in_{n}": v for n, v in arrays.items()}], core_ids=[0])
    return r.results[0]["out_0"].reshape(BATCH, SEQ, D)
```

```python
from contextlib import ExitStack

import concourse.bass as bass
from concourse import mybir

F32 = mybir.dt.float32
F32R = mybir.dt.float32r
ALU = mybir.AluOpType
ACT = mybir.ActivationFunctionType

P = 128
BATCH, SEQ, D = 16, 256, 256
TOKENS = BATCH * SEQ
BLOCK = 512
NBLK = TOKENS // BLOCK
TPB = BLOCK // P
SPB = BLOCK // SEQ
NTILE = TOKENS // P
KD = D // P
FF = 512
NEXP = 2
HT = NEXP * FF // P
DI = 512
NQ = DI // P
NH, HD = 8, 64
NS = 16
TAPS = 4
EPS = 1e-5

W_X, W_G, W_BC, W_DT, W_COLS = 0, DI, 2 * DI, 2 * DI + P, 2 * DI + P + NH
C_ROW = 32

(Q_WG, Q_B0, Q_CW, Q_CB, Q_DS, Q_NW, Q_DTB, Q_AL, Q_END) = (
    0, KD * 2, KD * 2 + HT, KD * 2 + HT + 5 * TAPS, KD * 2 + HT + 5 * TAPS + 5,
    KD * 2 + HT + 5 * TAPS + 5 + NQ, KD * 2 + HT + 5 * TAPS + 5 + 2 * NQ,
    KD * 2 + HT + 5 * TAPS + 5 + 2 * NQ + NH, KD * 2 + HT + 5 * TAPS + 5 + 2 * NQ + 2 * NH)
K_ID, K_TRI, K_SUF, K_MASK, K_NF, K_END = 0, 4 * P, 5 * P, 6 * P, 10 * P, 10 * P + 1

A_LOW, A_HIGH = 60.0, 28.7
FAST = 200.0


def macaron(nc, x, wa, wb, win, wout, params, consts, bout, out):
    ctx = ExitStack()
    with ctx:
        def sb(name, cols, dt=F32):
            return ctx.enter_context(nc.sbuf_tensor(name, [P, cols], dt))

        def sem(name):
            return ctx.enter_context(nc.semaphore(name))

        X = sb("X", NTILE * D)[:, :].rearrange("p (n d) -> p n d", d=D)
        wa_hi = sb("wa_hi", KD * HT * P, F32R)[:, :].rearrange("p (k n) -> p k n", k=KD)
        wa_lo = sb("wa_lo", KD * HT * P, F32R)[:, :].rearrange("p (k n) -> p k n", k=KD)
        wb_hi = sb("wb_hi", HT * D, F32R)[:, :].rearrange("p (k n) -> p k n", k=HT)
        wb_lo = sb("wb_lo", HT * D, F32R)[:, :].rearrange("p (k n) -> p k n", k=HT)
        wi_hi = sb("wi_hi", KD * W_COLS, F32R)[:, :].rearrange("p (k n) -> p k n", k=KD)
        wi_lo = sb("wi_lo", KD * W_COLS, F32R)[:, :].rearrange("p (k n) -> p k n", k=KD)
        wo_hi = sb("wo_hi", NQ * D, F32R)[:, :].rearrange("p (k n) -> p k n", k=NQ)
        wo_lo = sb("wo_lo", NQ * D, F32R)[:, :].rearrange("p (k n) -> p k n", k=NQ)
        wg_hi = sb("wg_hi", KD * 2, F32R)[:, :].rearrange("p (k n) -> p k n", k=KD)
        wg_lo = sb("wg_lo", KD * 2, F32R)[:, :].rearrange("p (k n) -> p k n", k=KD)
        prm = sb("prm", Q_END)
        cst = sb("cst", K_END)
        ident4 = cst[:, K_ID:K_ID + 4 * P]
        ident = cst[:, K_ID:K_ID + P]
        bo = sb("bo", 2 * D)
        xn = sb("xn", TPB * D)[:, :].rearrange("p (n d) -> p n d", d=D)
        xt_hi = sb("xt_hi", KD * BLOCK, F32R)[:, :].rearrange("p (k n) -> p k n", k=KD)
        xt_lo = sb("xt_lo", KD * BLOCK, F32R)[:, :].rearrange("p (k n) -> p k n", k=KD)
        n_wa, n_wb, n_wi, n_wo = KD * HT * P, HT * D, KD * W_COLS, NQ * D
        stage = sb("stage", n_wa + n_wb + n_wi + n_wo)
        st_wa = stage[:, 0:n_wa]
        st_wb = stage[:, n_wa:n_wa + n_wb]
        st_wi = stage[:, n_wa + n_wb:n_wa + n_wb + n_wi]
        st_wo = stage[:, n_wa + n_wb + n_wi:n_wa + n_wb + n_wi + n_wo]
        xs = stage[:, 0:NQ * BLOCK].rearrange("p (q n) -> p q n", q=NQ)
        gs = stage[:, NQ * BLOCK:2 * NQ * BLOCK].rearrange("p (q n) -> p q n", q=NQ)
        xd = stage[:, 2 * NQ * BLOCK:3 * NQ * BLOCK].rearrange("p (q n) -> p q n", q=NQ)
        scratch = sb("scratch", 2 * BLOCK)
        xbuf = sb("xbuf", TPB * D)
        xb = xbuf[:, :].rearrange("p (n d) -> p n d", d=D)
        xdt = [xbuf[:, n * DI:(n + 1) * DI] for n in range(2)]
        st6 = sb("st6", TPB * 6)[:, :].rearrange("p (n d) -> p n d", d=6)
        mv = sb("mv", TPB * 2)[:, :].rearrange("p (n d) -> p n d", d=2)
        mvm = sb("mvm", TPB * 2)[:, :].rearrange("p (n d) -> p n d", d=2)
        mv2 = sb("mv2", NTILE * 2)[:, :].rearrange("p (n d) -> p n d", d=2)
        veps = sb("veps", TPB)
        rstd = sb("rstd", TPB)
        rstd2 = sb("rstd2", NTILE)
        mhalf = sb("mhalf", TPB)
        logit = sb("logit", TPB * 2)[:, :].rearrange("p (n d) -> p n d", d=2)
        sel = sb("sel", TPB)
        m0h = sb("m0h", TPB)
        m1h = sb("m1h", TPB)
        ones = sb("ones", 1)
        dt_raw = sb("dt_raw", NTILE * NH)
        DEC = sb("DEC", 4 * NTILE * NH)
        dec4 = DEC[:, :].rearrange("p (k n) -> p k n", k=4)
        dec = sb("dec", 4 * TPB * NH)
        dec_b = dec[:, :].rearrange("p (k c h) -> p k c h", k=4, c=TPB)
        decay = [sb(f"decay{n}", 4 * P) for n in range(2)]
        M0 = sb("M0", NH * P)
        yg0 = sb("yg0", BLOCK)
        bsel = yg0[:, 0:D]
        sq0 = sb("sq0", BLOCK)
        hid = [scratch[:, 0:BLOCK], scratch[:, BLOCK:2 * BLOCK], sq0[:, :], M0[:, BLOCK:2 * BLOCK]]
        NHID = len(hid)
        scores = sb("scores", BLOCK)
        bt = sb("bt", BLOCK)
        part = bt[:, :].rearrange("p (n d) -> p n d", d=D)
        ct = sb("ct", BLOCK)
        bct = sb("bct", TPB * NS)
        bw = stage[:, (3 * NQ + 2) * BLOCK:(3 * NQ + 2) * BLOCK + SPB * P]
        cp = sb("cp", SPB * P)
        cpt = sb("cpt", SPB * P)
        hst = sb("hst", DI)
        yv = sb("yv", 1)
        yr = sb("yr", 1)
        eA = sb("eA", 4 * NH)
        with nc.sbuf_tensor("hid_hi", [P, HT * BLOCK], F32R) as hh, nc.sbuf_tensor("hid_lo", [P, HT * BLOCK], F32R) as hl:
            hid_hi = hh[:, :].rearrange("p (k n) -> p k n", k=HT)
            hid_lo = hl[:, :].rearrange("p (k n) -> p k n", k=HT)
        gated_hi, gated_lo = sb("gated_hi", 2 * BLOCK, F32R), sb("gated_lo", 2 * BLOCK, F32R)
        y_hi, y_lo = ([g[:, n * BLOCK:(n + 1) * BLOCK] for n in range(2)] for g in (gated_hi, gated_lo))
        xt_last = tuple(g[:, :].rearrange("p (k n) -> p k n", k=KD) for g in (gated_hi, gated_lo))
        M = [M0, sb("M1", NH * P)]
        yg = [yg0, sb("yg1", BLOCK)]
        sq = [sq0, sb("sq1", BLOCK)]
        ssq = [sb(f"ssq{n}", P) for n in range(2)]
        conv_space = sb("conv_space", 6 * BLOCK)
        raw = hid[0:2] + [conv_space[:, n * BLOCK:(n + 1) * BLOCK] for n in range(3)]
        acc = [stage[:, (3 * NQ + n) * BLOCK:(3 * NQ + n + 1) * BLOCK] for n in range(2)] + [
            conv_space[:, n * BLOCK:(n + 1) * BLOCK] for n in range(3, 6)]

        bank = [ctx.enter_context(nc.psum_tensor(f"bank{n}", [P, 512], F32)) for n in range(8)]
        ring, l2p, l1p = bank[0:2], bank[2:4], bank[4:6]
        gatep, dtp = bank[6], bank[7]
        gate_rows, dt_rows = ct[:, :], M0[:, 0:BLOCK]
        decp, pxp, hp, yp, op = bank[2:4], bank[4], bank[5], bank[6], bank[7]

        s_prm, s_cst, s_bo, s_wa, s_wb, s_wi, s_wo, s_out = (
            sem(n) for n in ("params_in", "consts_in", "biases_in", "wa_in", "wb_in", "wi_in", "wo_in", "stored"))
        s_wa = [s_wa, sem("wa_in1")]
        s_x = [sem(f"x_in{n}") for n in range(NBLK)]
        s_id = sem("identity_in")
        w_scaled, w_hi, w_lo = sem("w_scaled"), sem("w_hi"), sem("w_lo")
        s_const, bias_half = sem("const_set"), sem("bias_half")

        def Phase(name, events):
            return {e: sem(f"{name}_{e}") for e in events}

        norm_events = ("bn", "mv", "stats", "rstd", "xn", "xt", "xhi", "xlo")
        ffn_events = norm_events + (
            "gate_rows", "gate_sb", "gate", "gate_read", "picked", "masks", "l1", "act", "hhi", "hlo", "l2", "xb0", "xb",
            "half", "comb", "dt_rows", "dt_sb", "dt", "dt_read", "mvkept")
        fa = Phase("ffn1", ffn_events)
        fb = Phase("ffn2", ffn_events)

        def dve_stats(v, f, s, blk, mvs, wait, wait_rstd):
            wait()
            for t in range(TPB):
                ins = v.bn_stats(st6[:, t, :], X[:, blk * TPB + t, :])
            ins.then_inc(f["bn"], 1)
            v.wait_ge(f["bn"], s + 1)
            if wait_rstd:
                v.wait_ge(f["rstd"], s)
            v.memset(veps[:, :], EPS)
            for t in range(TPB):
                ins = v.bn_aggr(mvs[:, t, :], st6[:, t, :])
            ins.then_inc(f["mv"], 1)
            v.wait_ge(f["mv"], s + 1)
            v.tensor_tensor(veps[:, :], veps[:, :], mvs[:, :, 1], ALU.add).then_inc(f["stats"], 1)

        def pool_rstd(g, f, s, dst):
            g.wait_ge(f["stats"], s + 1)
            g.tensor_tensor(dst, veps[:, :], mhalf[:, :], ALU.pow).then_inc(f["rstd"], 1)

        def dve_apply(v, f, s, blk, mean, rs, first):
            v.wait_ge(f["rstd"], s + 1)
            if not first:
                v.wait_ge(f["xt"], 2 * s)
            for t in range(TPB):
                ins = v.tensor_scalar(xn[:, t, :], X[:, blk * TPB + t, :], mean(t), rs(t),
                                      ALU.subtract, ALU.mult)
            ins.then_inc(f["xn"], 1)

        def pe_turn(pe, f, s, first, banks=ring):
            pe.wait_ge(f["xn"], s + 1)
            for k in range(KD):
                if not first:
                    pe.wait_ge(f["xlo"], 2 * s - 1 + k)
                for t in range(TPB):
                    ins = pe.transpose(banks[k][:, t * P:(t + 1) * P], xn[:, t, k * P:(k + 1) * P], ident)
                ins.then_inc(f["xt"], 1)

        def act_hi(a, f, s, banks=ring, dst=xt_hi):
            for k in range(KD):
                a.wait_ge(f["xt"], 2 * s + k + 1)
                a.activation(dst[:, k, :], banks[k][:, :], ACT.Copy).then_inc(f["xhi"], 1)

        def dve_lo(v, f, s, banks=ring, hi=xt_hi, dst=xt_lo):
            for k in range(KD):
                v.wait_ge(f["xhi"], 2 * s + k + 1)
                v.tensor_tensor(dst[:, k, :], banks[k][:, :], hi[:, k, :].bitcast(F32),
                                ALU.subtract).then_inc(f["xlo"], 1)

        def product(pe, dst, lhs, rhs, ks):
            ks = list(ks)
            for n, k in enumerate(ks):
                pe.matmul(dst, lhs(0, k), rhs(0, k), start=(n == 0), stop=False)
                pe.matmul(dst, lhs(0, k), rhs(1, k), start=False, stop=False)
                ins = pe.matmul(dst, lhs(1, k), rhs(0, k), start=False, stop=(n == len(ks) - 1))
            return ins

        xt = (xt_hi, xt_lo)
        wa2, wb2, wi2, wo2, wg2 = (wa_hi, wa_lo), (wb_hi, wb_lo), (wi_hi, wi_lo), (wo_hi, wo_lo), (wg_hi, wg_lo)
        hid2, y2 = (hid_hi, hid_lo), (y_hi, y_lo)

        tail = Phase("dt", ("v", "av", "e", "eA", "u", "ln", "um1", "z", "rec", "q", "q2", "ez", "dt0", "dt",
                            "clip", "a1", "a2", "a", "dA", "cum", "P", "done"))
        PARTS = (0, NBLK - 2, NBLK)
        TC = TPB * NH
        late = sb("late", 2 * 2 * TC)

        class Part:
            def __init__(self, p):
                cols = slice(PARTS[p] * TC, PARTS[p + 1] * TC)
                self.n = cols.stop - cols.start
                own_space = late if p else stage[:, 2 * NQ * BLOCK:3 * NQ * BLOCK]
                self.v = dt_raw[:, cols]
                self.a, self.u = own_space[:, 0:self.n], own_space[:, self.n:2 * self.n]
                self.dA, self.dt, self.upto, self.after = (dec4[:, k, cols] for k in range(4))
                self.e, self.q, self.z, self.r = self.upto, self.after, self.dA, self.dt
                bank_of = hp if p else yp
                self.sums = [bank_of[:, 0:self.n], bank_of[:, self.n:2 * self.n]]

            def per_head(self, col):
                return eA[:, col * NH:(col + 1) * NH].unsqueeze(1).broadcast_to([P, self.n // NH, NH])

        parts = [Part(p) for p in range(2)]

        def by_head(ap):
            return ap.rearrange("p (n h) -> p n h", h=NH)

        def step(v, p, ins, s):
            ins.then_inc(s, 1)
            v.wait_ge(s, p + 1)

        def dve_bias(v, p):
            t = parts[p]
            v.wait_ge(fa["dt_read"], PARTS[p + 1])
            step(v, p, v.tensor_tensor(by_head(t.v), by_head(t.v), prm[:, Q_DTB:Q_DTB + NH].unsqueeze(1).broadcast_to(
                [P, t.n // NH, NH]), ALU.add), tail["v"])
            v.scalar_tensor_tensor(out=t.a, in0=t.v, scalar=-1.0, in1=t.v, op0=ALU.mult, op1=ALU.max).then_inc(tail["av"], 1)
            if p == 0:
                v.tensor_scalar(eA[:, 0:NH], prm[:, Q_AL:Q_AL + NH], A_LOW, None, ALU.min)
                step(v, p, v.tensor_scalar(eA[:, NH:2 * NH], prm[:, Q_AL:Q_AL + NH], A_LOW, 0.0, ALU.subtract, ALU.max),
                     tail["clip"])
                v.tensor_scalar(eA[:, NH:2 * NH], eA[:, NH:2 * NH], A_HIGH, None, ALU.min).then_inc(tail["clip"], 1)

        def dve_factors(v, p):
            t = parts[p]
            v.wait_ge(tail["e"], p + 1)
            step(v, p, v.tensor_scalar(t.u, t.e, 1.0, None, ALU.add), tail["u"])
            step(v, p, v.tensor_scalar(t.z, t.u, 1.0, None, ALU.is_equal), tail["z"])
            step(v, p, v.scalar_tensor_tensor(out=t.r, in0=t.u, scalar=1.0, in1=t.z, op0=ALU.subtract, op1=ALU.add),
                 tail["um1"])
            step(v, p, v.reciprocal(t.r, t.r), tail["rec"])
            v.tensor_tensor(t.z, t.z, t.e, ALU.mult).then_inc(tail["ez"], 1)

        def dve_dt(v, p):
            t = parts[p]
            v.wait_ge(tail["ln"], p + 1)
            step(v, p, v.tensor_tensor(t.q, t.q, t.e, ALU.mult), tail["q"])
            step(v, p, v.tensor_tensor(t.q, t.q, t.r, ALU.mult), tail["q2"])
            v.wait_ge(tail["ez"], p + 1)
            step(v, p, v.tensor_tensor(t.q, t.q, t.z, ALU.add), tail["dt0"])
            step(v, p, v.scalar_tensor_tensor(out=t.dt, in0=t.v, scalar=0.0, in1=t.q, op0=ALU.max, op1=ALU.add), tail["dt"])
            v.wait_ge(tail["eA"], 1)
            step(v, p, v.tensor_tensor(by_head(t.a), by_head(t.dt), t.per_head(2), ALU.mult), tail["a1"])
            step(v, p, v.scalar_tensor_tensor(out=by_head(t.a), in0=by_head(t.a), scalar=FAST, in1=t.per_head(3),
                                              op0=ALU.min, op1=ALU.mult), tail["a2"])
            v.tensor_scalar(t.a, t.a, FAST, None, ALU.min).then_inc(tail["a"], 1)

        def dve_dA(v, p):
            t = parts[p]
            v.wait_ge(tail["dA"], p + 1)
            v.tensor_scalar(t.dA, t.u, cst[:, K_NF:K_NF + 1], None, ALU.mult).then_inc(tail["done"], 1)

        def dve_part_there(v, p):
            v.wait_ge(tail["P"], 2 * p + 2)
            v.wait_ge(tail["done"], p + 1)

        def act_e(a, p):
            t = parts[p]
            a.wait_ge(tail["av"], p + 1)
            a.activation(t.e, t.a, ACT.Exp, scale=-1.0).then_inc(tail["e"], 1)
            if p == 0:
                a.wait_ge(tail["clip"], 2)
                a.activation(eA[:, 2 * NH:4 * NH], eA[:, 0:2 * NH], ACT.Exp).then_inc(tail["eA"], 1)

        def act_ln(a, p):
            t = parts[p]
            a.wait_ge(tail["u"], p + 1)
            a.activation(t.q, t.u, ACT.Ln).then_inc(tail["ln"], 1)

        def act_dA(a, p):
            t = parts[p]
            a.wait_ge(tail["a"], p + 1)
            a.activation(t.u, t.a, ACT.Exp, scale=-1.0).then_inc(tail["dA"], 1)

        def act_products(a, p):
            t = parts[p]
            a.wait_ge(tail["cum"], p + 1)
            a.activation(t.upto, t.sums[0], ACT.Exp, scale=-1.0).then_inc(tail["P"], 1)
            a.activation(t.after, t.sums[1], ACT.Exp, scale=-1.0).then_inc(tail["P"], 1)

        def pe_sums(pe, p):
            t = parts[p]
            pe.wait_ge(tail["a"], p + 1)
            pe.matmul(t.sums[0], cst[:, K_TRI:K_TRI + P], t.a, start=True, stop=True)
            pe.matmul(t.sums[1], cst[:, K_SUF:K_SUF + P], t.a, start=True, stop=True).then_inc(tail["cum"], 1)

        def own(dt, i):
            return 2 * i - 1 if dt else i

        def pe_gate(pe, f, i, dt, first):
            s = 0 if first else own(dt, i)
            pe.wait_ge(f["xlo"], 2 * s + 2)
            if not first:
                pe.wait_ge(f["gate_read"], i)
            product(pe, gatep[0:NEXP, :], lambda a, k: wg2[a][:, k, :], lambda a, k: xt[a][:, k, :],
                    range(KD)).then_inc(f["gate_rows"], 1)

        def pe_ffn(pe, f, i, dt, first, last):
            if dt and first:
                pe.wait_ge(w_lo, 1)
            if dt or not first:
                pe_gate(pe, f, i, dt, first)
            if dt and first:
                pe.wait_ge(w_lo, 3)
            for m in range(HT):
                if m == 1:
                    pe_rows_there(pe, f, "gate", i)
                if not dt and first and m == 2:
                    pe_out(pe, NTILE - 1, 1)
                if not (first and m < 2):
                    pe.wait_ge(f["act"], i * HT + m - 1)
                ins = product(pe, l1p[m % 2][:, :], lambda a, k: wa2[a][:, k, m * P:(m + 1) * P],
                              lambda a, k: xt[a][:, k, :], range(KD))
                ins.then_inc(f["l1"], 1)
                if m == 1:
                    pe_columns(pe, f, "gate", i, gatep, gate_rows, NEXP)
            if dt and first:
                pe.wait_ge(w_lo, 4)

            def second(t, e):
                if e == 0 and not (first and t < 2):
                    pe.wait_ge(f["comb"], i * TPB + t - 1)
                return product(pe, l2p[t % 2][:, e * D:(e + 1) * D],
                               lambda a, k: hid2[a][:, k, t * P:(t + 1) * P],
                               lambda a, k: wb2[a][:, k, :], range(4 * e, 4 * e + 4))

            pe.wait_ge(f["hlo"], i * HT + 4)
            second(0, 0)
            second(1, 0)
            if dt and not first:
                pe_turn(pe, f, 2 * i, False)
            if not dt and not last:
                pe_turn(pe, f, own(dt, i + 1), False)
            pe.wait_ge(f["hlo"], i * HT + 8)
            second(0, 1).then_inc(f["l2"], 1)
            if dt and not first:
                pe_dt(pe, f, 2 * i, i - 1)
            if dt and not last:
                pe_turn(pe, f, own(dt, i + 1), False)
            elif dt:
                pe_turn_mix(pe, 0, True)
            if dt and not first:
                pe_rows_there(pe, f, "dt", i - 1)
            second(1, 1).then_inc(f["l2"], 1)
            if dt and not first:
                pe_columns(pe, f, "dt", i - 1, dtp, dt_rows, NH)
            for t in range(2, TPB):
                second(t, 0)
                second(t, 1).then_inc(f["l2"], 1)

        def pe_columns(pe, f, what, b, bank, rows, n):
            for t in range(TPB):
                ins = pe.transpose(bank[:, t * n:(t + 1) * n], rows[0:n, t * P:(t + 1) * P], ident[0:n, 0:n])
            ins.then_inc(f[what], 1)

        def pe_rows_there(pe, f, what, b):
            pe.wait_ge(f[what + "_sb"], b + 1)

        def pe_dt(pe, f, s, b, xt=xt):
            pe.wait_ge(w_lo, 5)
            pe.wait_ge(f["xlo"], 2 * s + 2)
            pe.wait_ge(f["dt_read"], b)
            product(pe, dtp[0:NH, :], lambda a, k: wi2[a][:, k, W_DT:W_DT + NH], lambda a, k: xt[a][:, k, :],
                    range(KD)).then_inc(f["dt_rows"], 1)

        def act_rows(a, f, what, b, bank, rows, n):
            a.wait_ge(f[what + "_rows"], b + 1)
            a.activation(rows[0:n, :], bank[0:n, :], ACT.Copy).then_inc(f[what + "_sb"], 1)

        def act_ffn(a, f, i, dt, first, last):
            act_rows(a, f, "gate", i, gatep, gate_rows, NEXP)
            for m in range(HT + 1):
                if m < HT:
                    n = i * HT + m
                    a.wait_ge(f["l1"], n + 1)
                    if not (first and m < NHID):
                        a.wait_ge(f["hlo"], n - NHID + 1)
                    func = ACT.Gelu if m < HT // NEXP else ACT.Relu
                    a.activation(hid[m % NHID], l1p[m % 2][:, :], func,
                                 bias=prm[:, Q_B0 + m:Q_B0 + m + 1]).then_inc(f["act"], 1)
                if m:
                    if not dt and first and m == 1:
                        a.wait_ge(mx["fin"], NTILE)
                    a.wait_ge(f["act"], i * HT + m)
                    a.activation(hid_hi[:, m - 1, :], hid[(m - 1) % NHID], ACT.Copy).then_inc(f["hhi"], 1)
            if dt and last:
                act_e(a, 0)
            if dt and not first:
                act_hi(a, f, 2 * i)
                act_rows(a, f, "dt", i - 1, dtp, dt_rows, NH)
            if not last:
                act_hi(a, f, own(dt, i + 1))

        def dve_ffn(v, f, i, dt, first, last):
            if dt and last:
                dve_bias(v, 0)
            if dt and not first:
                dve_stats_mixer(v, f, i)
            v.wait_ge(f["gate"], i + 1)
            v.tensor_copy(logit, gatep[:, 0:2 * TPB].rearrange("p (n d) -> p n d", d=2)).then_inc(f["gate_read"], 1)
            v.wait_ge(f["gate_read"], i + 1)
            v.tensor_tensor(sel[:, :], logit[:, :, 0], logit[:, :, 1], ALU.is_ge).then_inc(f["picked"], 1)
            v.wait_ge(f["picked"], i + 1)
            if not first:
                v.wait_ge(f["xb"], i * TPB)
            v.tensor_scalar(m0h[:, :], sel[:, :], 0.5, None, ALU.mult)
            v.tensor_scalar(m1h[:, :], sel[:, :], -0.5, 0.5, ALU.mult, ALU.add).then_inc(f["masks"], 1)

            def lo(m):
                v.wait_ge(f["hhi"], i * HT + m + 1)
                v.tensor_tensor(hid_lo[:, m, :], hid[m % NHID], hid_hi[:, m, :].bitcast(F32),
                                ALU.subtract).then_inc(f["hlo"], 1)

            def combine(t):
                n = i * TPB + t
                v.wait_ge(f["l2"], n + 1)
                v.wait_ge(f["xb"], n + 1)
                v.scalar_tensor_tensor(out=part[:, t % 2, :], in0=l2p[t % 2][:, 0:D], scalar=m0h[:, t:t + 1],
                                       in1=xb[:, t, :], op0=ALU.mult, op1=ALU.add).then_inc(f["half"], 1)
                v.wait_ge(f["half"], n + 1)
                v.scalar_tensor_tensor(out=X[:, i * TPB + t, :], in0=l2p[t % 2][:, D:2 * D], scalar=m1h[:, t:t + 1],
                                       in1=part[:, t % 2, :], op0=ALU.mult, op1=ALU.add).then_inc(f["comb"], 1)

            if not last:
                dve_stats_own(v, f, own(dt, i + 1), i + 1)
            for m in range(0, 2):
                lo(m)
            for m in range(2, 4):
                lo(m)
            if dt and not first:
                dve_apply_mixer(v, f, 2 * i, i - 1)
            for m in range(4, 6):
                lo(m)
            if not dt and not last:
                dve_apply_own(v, f, own(dt, i + 1), i + 1)
            for m in range(6, 8):
                lo(m)
            if dt and not first:
                dve_lo(v, f, 2 * i)
            if dt and not last:
                dve_apply_own(v, f, own(dt, i + 1), i + 1)
            elif dt:
                v.wait_ge(f["xt"], 4 * i + 2)
                dve_mix_xn(v, 0, True)
            combine(0)
            if not last:
                dve_lo(v, f, own(dt, i + 1))
            elif dt:
                dve_xt_lo(v, 0)
            for t in range(1, TPB):
                combine(t)
                if dt and not first and t == 1:
                    dve_dt_read(v, f, i - 1)
                if dt and first and t < 3:
                    k = t - 1
                    v.wait_ge(w_hi, 5)
                    ins = v.tensor_tensor(wi_lo[:, k, :], st_wi[:, k * W_COLS:(k + 1) * W_COLS],
                                          wi_hi[:, k, :].bitcast(F32), ALU.subtract)
                    if t == 2:
                        ins.then_inc(w_lo, 1)
                if dt and last and t == 1:
                    dve_factors(v, 0)
                if dt and last and t == 2:
                    dve_dt(v, 0)

        def dve_stats_own(v, f, s, blk, first=False):
            def there():
                if f is fa:
                    if isinstance(blk, int):
                        v.wait_ge(s_x[blk], 16)
                    else:
                        for n in range(NBLK):
                            v.wait_ge(s_x[n], 16)
                else:
                    v.wait_ge(mx["fin"], (blk + 1) * TPB if isinstance(blk, int) else NTILE)
            dve_stats(v, f, s, blk, mv, there, not first)

        def dve_apply_own(v, f, s, blk, first=False):
            dve_apply(v, f, s, blk, lambda t: mv[:, t, 0:1], lambda t: rstd[:, t:t + 1], first)

        def dve_stats_mixer(v, f, i, s=None):
            b = i - 1
            dve_stats(v, f, 2 * i if s is None else s, b, mvm,
                      lambda: v.wait_ge(f["comb"], i * TPB), True)
            v.tensor_copy(mv2[:, bass.ds(b * TPB, TPB), :], mvm[:, :, :]).then_inc(f["mvkept"], 1)

        def dve_apply_mixer(v, f, s, b, first=False):
            v.wait_ge(f["mvkept"], b + 1)
            dve_apply(v, f, s, b, lambda t: mv2[:, b * TPB + t, 0:1],
                      lambda t: rstd2[:, bass.ds(b * TPB + t, 1)], first)

        def dve_dt_read(v, f, b):
            v.wait_ge(f["dt"], b + 1)
            v.tensor_copy(dt_raw[:, bass.ds(b * TPB * NH, TPB * NH)], dtp[:, 0:TPB * NH]).then_inc(f["dt_read"], 1)

        def pool_ffn(g, f, i, dt, first, last):
            if dt and not first:
                pool_rstd(g, f, 2 * i, rstd2[:, bass.ds((i - 1) * TPB, TPB)])
            if not last:
                pool_rstd(g, f, own(dt, i + 1), rstd[:, :])
            g.wait_ge(f["masks"], i + 1)
            for t in range(TPB):
                n = i * TPB + t
                if not first:
                    g.wait_ge(f["comb"], n - TPB + 1)
                if not (first and t == 0):
                    g.wait_ge(f["xb"], n)
                g.tensor_tensor(xb[:, t, :], X[:, i * TPB + t, :], bo[:, D:2 * D], ALU.add)
                g.tensor_scalar(bsel, bo[:, 0:D], m0h[:, t:t + 1], None, ALU.mult).then_inc(f["xb0"], 1)
                g.wait_ge(f["xb0"], n + 1)
                g.tensor_tensor(xb[:, t, :], xb[:, t, :], bsel, ALU.add).then_inc(f["xb"], 1)

        def blocks(eng, step):
            step(0, True, False)
            with eng.Fori(1, NBLK - 1) as i:
                step(i, False, False)
            step(NBLK - 1, False, True)

        mx = Phase("mix", ("xn", "xhi",
            "full0", "full1", "free0", "free1", "dec", "tap", "silu", "bcsilu", "xd", "bwcp", "px", "xdt", "decp",
            "scan", "mm0", "mm1", "hp", "hst", "yp", "ysum", "yg", "sq", "ssq0", "ssq", "yhi", "ylo", "op", "yv", "yr",
            "fin"))
        full, free, mm = (mx["full0"], mx["full1"]), (mx["free0"], mx["free1"]), (mx["mm0"], mx["mm1"])
        SLOTS = ["T0", "T1", "BC", "x0", "x1", "x2", "x3", "S", "BCT", "g0", "g1", "CPT", "g2", "g3"]
        CONVS = ["BC", "x0", "x1", "x2", "x3"]
        PER = len(SLOTS) // 2

        def slot(i, what):
            j = SLOTS.index(what)
            return j % 2, i * PER + j // 2

        def fill(pe, sl, first=False):
            b, n = sl
            if not first:
                pe.wait_ge(free[b], n)
            return ring[b], full[b]

        def filled(eng, sl):
            b, n = sl
            eng.wait_ge(full[b], n + 1)
            return ring[b], free[b]

        def emptied(eng, sl):
            b, n = sl
            eng.wait_ge(free[b], n + 1)

        def pe_inproj(pe, sl, col, first=False):
            dst, done = fill(pe, sl, first)
            product(pe, dst[:, :], lambda a, k: wi2[a][:, k, col:col + P],
                    lambda a, k: xt[a][:, k, :], range(KD)).then_inc(done, 1)

        def pe_turn_mix(pe, i, first):
            pe.wait_ge(mx["xn"], i + 1)
            for k in range(KD):
                dst, done = fill(pe, slot(i, f"T{k}"), first)
                for t in range(TPB):
                    ins = pe.transpose(dst[:, t * P:(t + 1) * P], xn[:, t, k * P:(k + 1) * P], ident)
                ins.then_inc(done, 1)

        def pe_conv_in(pe, i, n):
            if n == 0:
                for k in range(KD):
                    emptied(pe, slot(i, f"T{k}"))
            pe_inproj(pe, slot(i, CONVS[n]), W_X + (n - 1) * P if n else W_BC)

        def pe_decay(pe, i, c, first):
            for half in range(2):
                if c == 0 and half == 0:
                    pe.wait_ge(mx["dec"], i + 1)
                if not (first and c == 0):
                    pe.wait_ge(mx["scan"], (i * TPB + c) * 2 + half - 1)
                for h in range(4):
                    ins = pe.transpose(decp[half][:, h * P:(h + 1) * P],
                                       dec_b[:, 0, c, 4 * half + h:4 * half + h + 1].broadcast_to([P, P]), ident)
                ins.then_inc(mx["decp"], 1)

        def pe_px(pe, i, c, first):
            if c == 0:
                pe.wait_ge(mx["silu"], (i + 1) * NQ)
            if not (first and c == 0):
                pe.wait_ge(mx["xdt"], i * TPB + c)
            for q in range(NQ):
                ins = pe.transpose(pxp[:, q * P:(q + 1) * P], xs[:, q, c * P:(c + 1) * P], ident)
            ins.then_inc(mx["px"], 1)

        def pe_state(pe, i, s, first):
            c = 2 * s
            pe.wait_ge(mx["xdt"], i * TPB + c + 1)
            if s == 0:
                pe.wait_ge(mx["bwcp"], i + 1)
            if not (first and s == 0):
                pe.wait_ge(mx["hst"], i * SPB + s)
            pe.matmul(hp[:, :], bw[:, s * P:(s + 1) * P], xdt[c % 2], start=True, stop=True).then_inc(mx["hp"], 1)

        def pe_y(pe, i, c, first):
            n = i * TPB + c
            pe.wait_ge(mx["xdt"], n + 1)
            for half in range(2):
                pe.wait_ge(mm[half], n + 1)
            if not (first and c == 0):
                pe.wait_ge(mx["ysum"], n)
            if c % 2:
                pe.wait_ge(mx["hst"], i * SPB + c // 2 + 1)
                emptied(pe, slot(i, "CPT"))
            for q in range(NQ):
                if c % 2:
                    pe.matmul(yp[:, q * P:(q + 1) * P], hst[:, q * P:(q + 1) * P],
                              cpt[:, (c // 2) * P:(c // 2 + 1) * P], start=True, stop=False, skip_group_check=True)
                for h in range(2):
                    ins = pe.matmul(yp[h * HD:(h + 1) * HD, q * P:(q + 1) * P],
                                    xdt[c % 2][:, (2 * q + h) * HD:(2 * q + h + 1) * HD],
                                    M[c % 2][:, (2 * q + h) * P:(2 * q + h + 1) * P],
                                    start=(c % 2 == 0), stop=True, skip_group_check=True)
            ins.then_inc(mx["yp"], 1)

        def pe_out(pe, n, b, first=False):
            if not first:
                pe.wait_ge(mx["fin"], n)
            pe.wait_ge(mx["ylo"], n + 1)
            product(pe, op[:, 0:D], lambda a, k: y2[a][b][:, k * P:(k + 1) * P],
                    lambda a, k: wo2[a][:, k, :], range(NQ))
            pe.wait_ge(mx["ssq"], n + 1)
            pe.matmul(op[:, D:D + 1], ssq[b][:, :], ones[:, :], start=True, stop=True).then_inc(mx["op"], 1)

        def pe_bc(pe, i):
            dst, done = fill(pe, slot(i, "S"))
            dst_t, done_t = fill(pe, slot(i, "BCT"))
            pe.wait_ge(mx["bcsilu"], i + 1)
            for c in range(TPB):
                ins = pe.matmul(dst[:, c * P:(c + 1) * P], bt[0:NS, c * P:(c + 1) * P], ct[0:NS, c * P:(c + 1) * P],
                                start=True, stop=True)
            ins.then_inc(done, 1)
            for c in range(TPB):
                src = ct if c % 2 else bt
                ins = pe.transpose(dst_t[:, c * NS:(c + 1) * NS], src[0:NS, c * P:(c + 1) * P], ident[0:NS, 0:NS])
            ins.then_inc(done_t, 1)

        def pe_mix(pe, i, first, last):
            n0 = i * TPB
            pe_inproj(pe, slot(i, "g0"), W_G)
            pe_px(pe, i, 0, first)
            pe_inproj(pe, slot(i, "g1"), W_G + P)
            dst, done = fill(pe, slot(i, "CPT"))
            pe.wait_ge(mx["bwcp"], i + 1)
            for s in range(SPB):
                ins = pe.transpose(dst[:, s * P:(s + 1) * P], cp[:, s * P:(s + 1) * P], ident)
            ins.then_inc(done, 1)
            for c in range(TPB):
                if c + 1 < TPB:
                    pe_px(pe, i, c + 1, first)
                    pe_decay(pe, i, c + 1, first)
                if first and c == 2:
                    pe.wait_ge(tail["P"], 4)
                if c % 2 == 0:
                    pe_state(pe, i, c // 2, first)
                if c == 0:
                    for q in range(2, NQ):
                        pe_inproj(pe, slot(i, f"g{q}"), W_G + q * P)
                    if not last:
                        pe_turn_mix(pe, i + 1, False)
                elif c < 3 and not last:
                    pe_conv_in(pe, i + 1, 2 * c - 1)
                pe_y(pe, i, c, first)
                if not (first and c == 0):
                    pe_out(pe, n0 + c - 1, (c - 1) % 2, first and c == 1)
                if 0 < c < 3 and not last:
                    pe_conv_in(pe, i + 1, 2 * c)
                if first and c == 1:
                    pe.wait_ge(mx["hst"], 1)
                    pe_sums(pe, 1)
                if c == 3 and not last:
                    pe_bc(pe, i + 1)
                    pe_decay(pe, i + 1, 0, False)
                if c == 0 and not last:
                    pe_conv_in(pe, i + 1, 0)
                if c == 1 and last:
                    emptied(pe, slot(i, "g2"))
                    emptied(pe, slot(i, "g3"))
                    pe_turn(pe, fb, 0, True)
            if last:
                pe.wait_ge(mx["ysum"], NTILE)
                pe_gate(pe, fb, 0, False, True)

        def conv_rows(n):
            return slice(0, C_ROW + NS) if n == 0 else slice(0, P)

        def tap_count(i, n, back):
            return i * 5 * 3 + (n // 2 * 6 + (back - 1) * 2 + n % 2 + 1 if n < 4 else 12 + back)

        def act_raw(a, i, n, first):
            src, done = filled(a, slot(i, CONVS[n]))
            r = conv_rows(n)
            if not first:
                if n == 0:
                    a.wait_ge(mx["bcsilu"], i)
                else:
                    a.wait_ge(mx["silu"], (i - 1) * NQ + n)
            cw = Q_CW + n * TAPS
            a.activation(raw[n][r, :], src[r, :], ACT.Copy)
            a.activation(acc[n][r, :], src[r, :], ACT.Identity, bias=prm[r, Q_CB + n:Q_CB + n + 1],
                         scale=prm[r, cw + 3:cw + 4]).then_inc(done, 1)

        def dve_tap(v, i, n, back):
            if back == 1:
                emptied(v, slot(i, CONVS[n]))
            else:
                v.wait_ge(mx["tap"], tap_count(i, n, back - 1))
            r = conv_rows(n)
            rows = raw[n][r, :].rearrange("p (s t) -> p s t", s=SPB)
            accs = acc[n][r, :].rearrange("p (s t) -> p s t", s=SPB)
            w = Q_CW + n * TAPS + 3 - back
            v.scalar_tensor_tensor(out=accs[:, :, back:], in0=rows[:, :, 0:SEQ - back], scalar=prm[r, w:w + 1],
                                   in1=accs[:, :, back:], op0=ALU.mult, op1=ALU.add).then_inc(mx["tap"], 1)

        def act_silu_bc(a, i, first):
            a.wait_ge(mx["tap"], tap_count(i, 0, 3))
            if not first:
                b, n = slot(i - 1, "BCT")
                a.wait_ge(full[b], n + 1)
            a.activation(bt[0:NS, :], acc[0][0:NS, :], ACT.Silu)
            a.activation(ct[0:NS, :], acc[0][C_ROW:C_ROW + NS, :], ACT.Silu).then_inc(mx["bcsilu"], 1)

        def act_silu_x(a, i, q, first):
            a.wait_ge(mx["tap"], tap_count(i, 1 + q, 3))
            if not first:
                if q == 0:
                    a.wait_ge(mx["px"], i * TPB)
                a.wait_ge(mx["xd"], (i - 1) * NQ + q + 1)
            a.activation(xs[:, q, :], acc[1 + q], ACT.Silu).then_inc(mx["silu"], 1)

        def act_xd(a, i, q, first):
            if not first and q == 0:
                a.wait_ge(mx["ysum"], i * TPB)
            a.wait_ge(mx["silu"], i * NQ + q + 1)
            a.activation(xd[:, q, :], xs[:, q, :], ACT.Copy, scale=prm[:, Q_DS + q:Q_DS + q + 1]).then_inc(mx["xd"], 1)

        def act_gate(a, i, q, first):
            src, done = filled(a, slot(i, f"g{q}"))
            if not first and q == 0:
                a.wait_ge(mx["yg"], i * TPB)
            a.activation(gs[:, q, :], src[:, :], ACT.Silu).then_inc(done, 1)

        def act_copy(a, i, what, dst, cols, wait):
            src, done = filled(a, slot(i, what))
            wait()
            a.activation(dst, src[:, 0:cols], ACT.Copy).then_inc(done, 1)

        def act_out(a, i, c, first):
            n = i * TPB + c
            if not (first and c < 2):
                a.wait_ge(mx["ssq"], n - 1)
            a.wait_ge(mx["yg"], n + 1)
            a.activation(sq[c % 2][:, :], yg[c % 2][:, :], ACT.Square).then_inc(mx["sq"], 1)
            if not (first and c < 2):
                a.wait_ge(mx["op"], n - 1)
            a.activation(y_hi[c % 2], yg[c % 2][:, :], ACT.Copy).then_inc(mx["yhi"], 1)

        def act_xt_hi(a, i, first):
            for k in range(KD):
                src, _ = filled(a, slot(i, f"T{k}"))
                if k == 0 and not first:
                    b, n = slot(i - 1, "g3")
                    a.wait_ge(full[b], n + 1)
                a.activation(xt_hi[:, k, :], src[:, :], ACT.Copy).then_inc(mx["xhi"], 1)

        def dve_xt_lo(v, i):
            for k in range(KD):
                v.wait_ge(mx["xhi"], 2 * i + k + 1)
                b, _ = slot(i, f"T{k}")
                v.tensor_tensor(xt_lo[:, k, :], ring[b][:, :], xt_hi[:, k, :].bitcast(F32),
                                ALU.subtract).then_inc(free[b], 1)

        def act_ahead(a, i, c, first):
            if c == 0:
                act_xt_hi(a, i, first)
                act_raw(a, i, 0, first)
            elif c < 3:
                act_raw(a, i, 2 * c, first)
                if c == 2:
                    act_silu_bc(a, i, first)
            else:
                for q in range(NQ - 1):
                    act_silu_x(a, i, q, first)

        def act_bc(a, i, first):
            def scores_free():
                if not first:
                    for half in range(2):
                        a.wait_ge(mm[half], i * TPB)
            act_copy(a, i, "S", scores[:, :], BLOCK, scores_free)

            def bct_free():
                if not first:
                    a.wait_ge(mx["bwcp"], i)
            act_copy(a, i, "BCT", bct[:, :], TPB * NS, bct_free)

        def act_mix(a, i, first, last):
            act_silu_x(a, i, NQ - 1, first)
            if first:
                a.wait_ge(tail["done"], 1)
            act_gate(a, i, 0, first)
            act_gate(a, i, 1, first)

            def cpt_free():
                if not first:
                    a.wait_ge(mx["yp"], i * TPB)
            act_copy(a, i, "CPT", cpt[:, :], SPB * P, cpt_free)
            for q in range(NQ):
                act_xd(a, i, q, first)
            act_gate(a, i, 2, first)
            act_gate(a, i, 3, first)
            if first:
                act_e(a, 1)
            for c in range(TPB):
                if c == 0 and not last:
                    act_ahead(a, i + 1, c, False)
                elif c < 3 and not last:
                    act_raw(a, i + 1, 2 * c - 1, False)
                elif not last:
                    act_ahead(a, i + 1, c, False)
                act_out(a, i, c, first)
                if first and c == 0:
                    act_ln(a, 1)
                if c == 3 and not last:
                    act_bc(a, i + 1, False)
                if 0 < c < 3 and not last:
                    act_ahead(a, i + 1, c, False)
                if first and c == 1:
                    act_dA(a, 1)
                    act_products(a, 1)
                if c == 1 and last:
                    act_hi(a, fb, 0)

        def dve_scan_half(v, i, c, half, first):
            n = (i * TPB + c) * 2 + half
            v.wait_ge(mx["decp"], n + 1)
            if not (first and c == 0):
                v.wait_ge(mm[half], i * TPB + c)
            v.tensor_tensor_scan(decay[half][:, :], decp[half][:, :], ident4, 0.0,
                                 ALU.mult, ALU.add).then_inc(mx["scan"], 1)

        DVE_HALVES = ((0, 1), (0,), (0,), ())
        POOL_HALVES = ((), (1,), (1,), (0, 1))

        def matrix(eng, i, c, half, first):
            n = i * TPB + c
            if c == 0:
                emptied(eng, slot(i, "S"))
            if not (first and c < 2):
                eng.wait_ge(mx["yp"], n - 1)
            eng.wait_ge(mx["scan"], 2 * n + half + 1)
            eng.tensor_tensor(M[c % 2][:, half * 4 * P:(half + 1) * 4 * P].rearrange("p (h t) -> p h t", h=4),
                              decay[half][:, :].rearrange("p (h t) -> p h t", h=4),
                              scores[:, c * P:(c + 1) * P].unsqueeze(1).broadcast_to([P, 4, P]),
                              ALU.mult).then_inc(mm[half], 1)

        def dve_xdt(v, i, c, first):
            n = i * TPB + c
            v.wait_ge(mx["px"], n + 1)
            if not (first and c < 2):
                v.wait_ge(mx["yp"], n - 1)
            v.tensor_tensor(xdt[c % 2].rearrange("p (h d) -> p h d", h=NH),
                            pxp[:, :].rearrange("p (h d) -> p h d", h=NH),
                            dec_b[:, 1, c, :].unsqueeze(2).broadcast_to([P, NH, HD]), ALU.mult).then_inc(mx["xdt"], 1)

        def dve_scaled_bc(v, i, first):
            emptied(v, slot(i, "BCT"))
            if not first:
                v.wait_ge(mx["hp"], i * SPB)
            for s in range(SPB):
                for dst, c, kind in ((bw, 2 * s, 3), (cp, 2 * s + 1, 2)):
                    ins = v.tensor_tensor(dst[:, s * P:(s + 1) * P].rearrange("p (h n) -> p h n", h=NH),
                                          bct[:, c * NS:(c + 1) * NS].unsqueeze(1).broadcast_to([P, NH, NS]),
                                          dec_b[:, kind, c, :].unsqueeze(2).broadcast_to([P, NH, NS]), ALU.mult)
            ins.then_inc(mx["bwcp"], 1)

        def dve_state(v, i, s, first):
            v.wait_ge(mx["hp"], i * SPB + s + 1)
            if not (first and s == 0):
                v.wait_ge(mx["yp"], i * TPB + 2 * s)
            v.tensor_tensor(hst[:, :], hp[:, :], cst[:, K_MASK:K_MASK + DI], ALU.mult).then_inc(mx["hst"], 1)

        def dve_y(v, i, c, first):
            n = i * TPB + c
            if c == 0:
                v.wait_ge(mx["xd"], (i + 1) * NQ)
            if not (first and c < 2):
                v.wait_ge(mx["sq"], n - 1)
                v.wait_ge(mx["yhi"], n - 1)
                v.wait_ge(mx["ylo"], n - 1)
            v.wait_ge(mx["yp"], n + 1)
            here = slice(c * P, (c + 1) * P)
            y4 = yg[c % 2][:, :].rearrange("p (q t) -> p q t", q=NQ)
            v.tensor_tensor(y4, yp[:, :].rearrange("p (q t) -> p q t", q=NQ), xd[:, :, here],
                            ALU.add).then_inc(mx["ysum"], 1)
            v.wait_ge(mx["ysum"], n + 1)
            if c == 0:
                emptied(v, slot(i, "g3"))
            v.tensor_tensor(y4, y4, gs[:, :, here], ALU.mult).then_inc(mx["yg"], 1)

        def dve_mean_square(v, n, first=False):
            if not first:
                v.wait_ge(mx["yr"], n)
            v.wait_ge(mx["op"], n + 1)
            v.tensor_scalar(yv[:, :], op[:, D:D + 1], 1.0 / DI, EPS, ALU.mult, ALU.add).then_inc(mx["yv"], 1)

        def dve_final(v, n):
            v.wait_ge(mx["yr"], n + 1)
            v.scalar_tensor_tensor(out=X[:, n, :], in0=op[:, 0:D], scalar=yr[:, :], in1=X[:, n, :],
                                   op0=ALU.mult, op1=ALU.add).then_inc(mx["fin"], 1)

        def pool_rms(g, n, first=False):
            if not first:
                g.wait_ge(mx["fin"], n)
            g.wait_ge(mx["yv"], n + 1)
            g.tensor_tensor(yr[:, :], yv[:, :], mhalf[:, 0:1], ALU.pow).then_inc(mx["yr"], 1)

        def pool_out(g, i, c, first):
            n, b = i * TPB + c, c % 2
            if c:
                pool_rms(g, n - 1, first and c == 1)
            g.wait_ge(mx["sq"], n + 1)
            g.tensor_tensor(sq[b][:, 0:2 * P], sq[b][:, 0:2 * P], sq[b][:, 2 * P:4 * P], ALU.add).then_inc(mx["ssq0"], 1)
            if not (first and c < 2):
                g.wait_ge(mx["op"], n - 1)
            g.wait_ge(mx["yhi"], n + 1)
            g.tensor_tensor(y_lo[b], yg[b][:, :], y_hi[b].bitcast(F32), ALU.subtract).then_inc(mx["ylo"], 1)
            g.wait_ge(mx["ssq0"], n + 1)
            g.tensor_tensor(ssq[b][:, :], sq[b][:, 0:P], sq[b][:, P:2 * P], ALU.add).then_inc(mx["ssq"], 1)

        def pool_mix(g, i, first, last):
            n0 = i * TPB
            if last:
                pool_rstd(g, fb, 0, rstd[:, :])
            for c in range(TPB):
                if c + 1 < TPB:
                    for half in POOL_HALVES[c + 1]:
                        matrix(g, i, c + 1, half, first)
                if c == 0 and not first:
                    pool_rms(g, n0 - 1)
                pool_out(g, i, c, first)
            if last:
                pool_rms(g, n0 + 3)

        def dve_dec(v, i, first):
            if not first:
                v.wait_ge(mx["bwcp"], i)
                v.wait_ge(mx["decp"], i * TPB * 2)
            v.tensor_copy(dec[:, :].rearrange("p (k n) -> p k n", k=4),
                          dec4[:, :, bass.ds(i * TPB * NH, TPB * NH)]).then_inc(mx["dec"], 1)
            v.wait_ge(mx["dec"], i + 1)

        def dve_mix_xn(v, i, first):
            if not first:
                filled(v, slot(i - 1, "T1"))
            for t in range(TPB):
                ins = v.tensor_scalar(xn[:, t, :], X[:, i * TPB + t, :], mv2[:, i * TPB + t, 0:1],
                                      rstd2[:, bass.ds(i * TPB + t, 1)], ALU.subtract, ALU.mult)
            ins.then_inc(mx["xn"], 1)

        MEAN_SQUARE_AFTER, FINAL_AFTER = {1: 1, 2: 1, 3: 3}, {1: 2, 2: 2}

        def dve_mix(v, i, first, last):
            n0 = i * TPB
            if not first:
                dve_scan_half(v, i, 0, 0, first)
                dve_scan_half(v, i, 0, 1, first)
                dve_final(v, n0 - 2)
            dve_scaled_bc(v, i, first)
            dve_xdt(v, i, 0, first)
            for half in DVE_HALVES[0]:
                matrix(v, i, 0, half, first)
            if not last:
                dve_mix_xn(v, i + 1, False)
            else:
                dve_stats_own(v, fb, 0, 0, True)
            for c in range(TPB):
                if c + 1 < TPB:
                    dve_xdt(v, i, c + 1, first)
                    dve_scan_half(v, i, c + 1, 0, first)
                    dve_scan_half(v, i, c + 1, 1, first)
                if c == 1 and not first:
                    dve_final(v, n0 - 1)
                if c % 2 == 0:
                    dve_state(v, i, c // 2, first)
                if c + 1 < TPB:
                    for half in DVE_HALVES[c + 1]:
                        matrix(v, i, c + 1, half, first)
                if c == 0 and not last:
                    dve_xt_lo(v, i + 1)
                if c == 3 and not last:
                    dve_dec(v, i + 1, False)
                if first and c == 1:
                    dve_dt(v, 1)
                dve_y(v, i, c, first)
                if first and c == 0:
                    dve_factors(v, 1)
                if first and c == 2:
                    dve_dA(v, 1)
                if first and c == 3:
                    dve_part_there(v, 1)
                if c == 0 and not first:
                    dve_mean_square(v, n0 - 1)
                if c:
                    tiles = ((0, 1), (2, 3), (4,))[c - 1]
                    for back in range(1, TAPS):
                        if not last:
                            for tile in tiles:
                                dve_tap(v, i + 1, tile, back)
                        if back == MEAN_SQUARE_AFTER[c]:
                            dve_mean_square(v, n0 + c - 1, first and c == 1)
                        elif back == FINAL_AFTER.get(c):
                            dve_final(v, n0 + c - 1)
                if c == 0 and last:
                    filled(v, slot(i, "T1"))
                    dve_apply_own(v, fb, 0, 0, True)
                if c == 2 and last:
                    dve_lo(v, fb, 0)
            if last:
                dve_final(v, n0 + 2)
                dve_mean_square(v, n0 + 3)
                dve_final(v, n0 + 3)

        block = ctx.enter_context(nc.Block())

        @block.sync
        def _(sp):
            xv = x.rearrange("(i t p) d -> i p t d", t=TPB, p=P)
            ov = out.rearrange("(i t p) d -> i p t d", t=TPB, p=P)
            sp.dma_start(X[:, 0:TPB, :], xv[0]).then_inc(s_x[0], 16)
            sp.dma_start(prm[:, :], params).then_inc(s_prm, 16)
            sp.dma_start(cst[:, 0:P], consts[:, 0:P]).then_inc(s_id, 16)
            for k in range(KD):
                half = slice(k * HT * P, (k + 1) * HT * P)
                sp.dma_start(st_wa[:, half], wa[:, half]).then_inc(s_wa[k], 16)
            sp.dma_start(X[:, TPB:2 * TPB, :], xv[1]).then_inc(s_x[1], 16)
            sp.dma_start(st_wb, wb).then_inc(s_wb, 16)
            sp.dma_start(bo[:, :], bout).then_inc(s_bo, 16)
            sp.dma_start(st_wi, win).then_inc(s_wi, 16)
            sp.dma_start(cst[:, P:K_END], consts[:, P:K_END]).then_inc(s_cst, 16)
            sp.dma_start(st_wo, wout).then_inc(s_wo, 16)
            for n in range(2, NBLK):
                sp.dma_start(X[:, n * TPB:(n + 1) * TPB, :], xv[n]).then_inc(s_x[n], 16)
            with sp.Fori(0, NBLK) as i:
                sp.wait_ge(fb["comb"], i * TPB + TPB)
                sp.dma_start(ov[i], X[:, bass.ds(i * TPB, TPB), :]).then_inc(s_out, 16)
            sp.wait_ge(s_out, 16 * NBLK)

        @block.gpsimd
        def _(g):
            g.memset(mhalf[:, :], -0.5).then_inc(s_const, 1)
            g.memset(ones[:, :], 1.0).then_inc(s_const, 1)
            g.wait_ge(s_const, 2)
            pool_rstd(g, fa, 0, rstd[:, :])

            g.wait_ge(s_bo, 16)
            g.tensor_tensor(bo[:, 0:D], bo[:, 0:D], bo[:, D:2 * D], ALU.subtract).then_inc(bias_half, 1)
            g.wait_ge(bias_half, 1)
            g.tensor_scalar(bo[:, D:2 * D], bo[:, D:2 * D], 0.5, None, ALU.mult).then_inc(bias_half, 1)
            g.wait_ge(s_wo, 16)
            g.wait_ge(s_prm, 16)
            for q in range(NQ):
                ins = g.tensor_scalar(st_wo[:, q * D:(q + 1) * D], st_wo[:, q * D:(q + 1) * D],
                                      prm[:, Q_NW + q:Q_NW + q + 1], None, ALU.mult)
            ins.then_inc(w_scaled, 1)
            g.wait_ge(bias_half, 2)
            blocks(g, lambda i, first, last: pool_ffn(g, fa, i, True, first, last))
            pool_rstd(g, fa, 2 * NBLK - 1, rstd2[:, (NBLK - 1) * TPB:NTILE])
            blocks(g, lambda i, first, last: pool_mix(g, i, first, last))
            blocks(g, lambda i, first, last: pool_ffn(g, fb, i, False, first, last))

        @block.scalar
        def _(a):
            a.wait_ge(s_prm, 16)
            a.activation(wg_hi.rearrange("p k n -> p (k n)"), prm[:, Q_WG:Q_WG + KD * 2], ACT.Copy).then_inc(w_hi, 1)
            a.wait_ge(s_wa[0], 16)
            a.activation(wa_hi[:, 0, :], st_wa[:, 0:HT * P], ACT.Copy).then_inc(w_hi, 1)
            act_hi(a, fa, 0)
            a.wait_ge(s_wa[1], 16)
            a.activation(wa_hi[:, 1, :], st_wa[:, HT * P:KD * HT * P], ACT.Copy).then_inc(w_hi, 1)

            def hi(dst, src):
                a.activation(dst.rearrange("p k n -> p (k n)"), src, ACT.Copy).then_inc(w_hi, 1)

            a.wait_ge(s_wb, 16)
            hi(wb_hi, st_wb)
            act_ffn(a, fa, 0, True, True, False)
            a.wait_ge(s_wi, 16)
            hi(wi_hi, st_wi)
            a.wait_ge(w_scaled, 1)
            hi(wo_hi, st_wo)
            with a.Fori(1, NBLK - 1) as i:
                act_ffn(a, fa, i, True, False, False)
            act_ffn(a, fa, NBLK - 1, True, False, True)
            act_xt_hi(a, 0, True)
            act_ln(a, 0)
            act_dA(a, 0)
            act_raw(a, 0, 0, True)
            act_products(a, 0)
            act_raw(a, 0, 1, True)
            act_raw(a, 0, 2, True)
            act_raw(a, 0, 3, True)
            act_raw(a, 0, 4, True)
            act_hi(a, fa, 2 * NBLK - 1, l1p, xt_last[0])
            act_silu_bc(a, 0, True)
            act_silu_x(a, 0, 0, True)
            act_rows(a, fa, "dt", NBLK - 1, dtp, dt_rows, NH)
            act_bc(a, 0, True)
            for q in range(1, NQ - 1):
                act_silu_x(a, 0, q, True)
            blocks(a, lambda i, first, last: act_mix(a, i, first, last))
            blocks(a, lambda i, first, last: act_ffn(a, fb, i, False, first, last))

        @block.vector
        def _(v):
            dve_stats_own(v, fa, 0, 0, True)
            v.wait_ge(s_prm, 16)
            v.wait_ge(w_hi, 1)
            v.tensor_tensor(wg_lo.rearrange("p k n -> p (k n)"), prm[:, Q_WG:Q_WG + KD * 2],
                            wg_hi.rearrange("p k n -> p (k n)").bitcast(F32), ALU.subtract).then_inc(w_lo, 1)
            dve_apply_own(v, fa, 0, 0, True)
            for k in range(KD):
                v.wait_ge(w_hi, k + 2)
                v.tensor_tensor(wa_lo[:, k, :], st_wa[:, k * HT * P:(k + 1) * HT * P], wa_hi[:, k, :].bitcast(F32),
                                ALU.subtract).then_inc(w_lo, 1)
                if k == 0:
                    dve_lo(v, fa, 0)

            def lo(dst, hi, src, n):
                v.wait_ge(w_hi, n)
                v.tensor_tensor(dst.rearrange("p k n -> p (k n)"), src,
                                hi.rearrange("p k n -> p (k n)").bitcast(F32), ALU.subtract).then_inc(w_lo, 1)

            lo(wb_lo, wb_hi, st_wb, 4)
            dve_ffn(v, fa, 0, True, True, False)
            lo(wo_lo, wo_hi, st_wo, 6)
            with v.Fori(1, NBLK - 1) as i:
                dve_ffn(v, fa, i, True, False, False)
            dve_ffn(v, fa, NBLK - 1, True, False, True)
            dve_stats_mixer(v, fa, NBLK, 2 * NBLK - 1)
            dve_dA(v, 0)
            dve_part_there(v, 0)
            dve_dec(v, 0, True)
            dve_tap(v, 0, 0, 1)
            dve_tap(v, 0, 1, 1)
            filled(v, slot(0, "T1"))
            dve_apply_mixer(v, fa, 2 * NBLK - 1, NBLK - 1)
            for back in range(2, TAPS):
                dve_tap(v, 0, 0, back)
                dve_tap(v, 0, 1, back)
            dve_tap(v, 0, 2, 1)
            dve_lo(v, fa, 2 * NBLK - 1, l1p, *xt_last)
            dve_tap(v, 0, 3, 1)
            dve_tap(v, 0, 2, 2)
            dve_tap(v, 0, 3, 2)
            dve_tap(v, 0, 2, 3)
            dve_tap(v, 0, 3, 3)
            for back in range(1, TAPS):
                dve_tap(v, 0, 4, back)
            dve_scan_half(v, 0, 0, 0, True)
            dve_scan_half(v, 0, 0, 1, True)
            dve_dt_read(v, fa, NBLK - 1)
            dve_bias(v, 1)
            blocks(v, lambda i, first, last: dve_mix(v, i, first, last))
            blocks(v, lambda i, first, last: dve_ffn(v, fb, i, False, first, last))

        @block.tensor
        def _(pe):
            pe.wait_ge(s_id, 16)
            pe_turn(pe, fa, 0, True)
            pe_ffn(pe, fa, 0, True, True, False)
            with pe.Fori(1, NBLK - 1) as i:
                pe_ffn(pe, fa, i, True, False, False)
            pe_ffn(pe, fa, NBLK - 1, True, False, True)
            pe.wait_ge(w_lo, 6)
            pe.wait_ge(s_cst, 16)
            pe.wait_ge(s_const, 2)
            pe_conv_in(pe, 0, 0)
            pe_sums(pe, 0)
            for n in range(1, 5):
                pe_conv_in(pe, 0, n)
            pe_turn(pe, fa, 2 * NBLK - 1, False, l1p)
            pe_decay(pe, 0, 0, True)
            pe_dt(pe, fa, 2 * NBLK - 1, NBLK - 1, xt_last)
            pe_bc(pe, 0)
            pe_rows_there(pe, fa, "dt", NBLK - 1)
            pe_columns(pe, fa, "dt", NBLK - 1, dtp, dt_rows, NH)
            blocks(pe, lambda i, first, last: pe_mix(pe, i, first, last))
            blocks(pe, lambda i, first, last: pe_ffn(pe, fb, i, False, first, last))


def kernel(**inputs):
    import numpy as np
    import concourse.bacc as bacc
    from concourse.bass_utils import run_bass_kernel_spmd

    a = {n.replace("L0_", ""): np.asarray(v) for n, v in inputs.items()}
    f = np.float32

    def tiles(w, k):
        return np.ascontiguousarray(w.reshape(k, P, -1).transpose(1, 0, 2).reshape(P, -1))

    def rows(v):
        return np.broadcast_to(v.reshape(1, -1), (P, v.size))

    wa = tiles(np.concatenate([a["ffn_W0a"], a["ffn_W1a"]]).T, KD)
    wb = tiles(np.concatenate([a["ffn_W0b"].T, a["ffn_W1b"].T]), HT)
    w = a["attn_W_in"]
    wi = np.zeros((D, W_COLS), f)
    wi[:, W_X:W_X + DI] = w[:, DI:2 * DI]
    wi[:, W_G:W_G + DI] = w[:, 0:DI]
    wi[:, W_BC:W_BC + NS] = w[:, 2 * DI:2 * DI + NS]
    wi[:, W_BC + C_ROW:W_BC + C_ROW + NS] = w[:, 2 * DI + NS:2 * DI + 2 * NS]
    wi[:, W_DT:W_DT + NH] = w[:, 2 * DI + 2 * NS:]
    win = tiles(wi, KD)
    wout = tiles(a["attn_W_out"], NQ)

    prm = np.zeros((P, Q_END), f)
    prm[:, Q_WG:Q_WG + 2 * KD] = tiles(a["ffn_Wg"].T, KD)
    prm[:, Q_B0:Q_B0 + HT] = np.concatenate([a["ffn_b0a"], a["ffn_b1a"]]).reshape(HT, P).T
    cw, cb = a["attn_conv_w"], a["attn_conv_b"]
    for n in range(5):
        for at, lo, hi in ([(0, DI, DI + NS), (C_ROW, DI + NS, DI + 2 * NS)] if n == 0 else
                           [(0, (n - 1) * P, n * P)]):
            prm[at:at + hi - lo, Q_CW + n * TAPS:Q_CW + (n + 1) * TAPS] = cw[lo:hi]
            prm[at:at + hi - lo, Q_CB + n] = cb[lo:hi]
    prm[:, Q_DS:Q_DS + NQ] = np.repeat(a["attn_D_skip"], HD).reshape(NQ, P).T
    prm[:, Q_NW:Q_NW + NQ] = a["attn_norm_w"].reshape(NQ, P).T
    prm[:, Q_DTB:Q_DTB + NH] = rows(a["attn_dt_bias"])
    prm[:, Q_AL:Q_AL + NH] = rows(a["attn_A_log"])
    bout = np.concatenate([rows(a["ffn_b0b"]), rows(a["ffn_b1b"])], axis=1)

    cst = np.zeros((P, K_END), f)
    cst[:, K_ID:K_ID + 4 * P] = np.tile(np.eye(P, dtype=f), (1, 4))
    cst[:, K_TRI:K_TRI + P] = np.triu(np.ones((P, P), f))
    cst[:, K_SUF:K_SUF + P] = np.tril(np.ones((P, P), f), -1)
    cst[:, K_MASK:K_MASK + DI] = np.kron(np.eye(NH, dtype=f), np.ones((NS, HD), f))
    cst[1:, K_NF] = 1.0

    arrays = {"x": np.ascontiguousarray(a["attn_hidden_states"].reshape(TOKENS, D)), "wa": wa, "wb": wb,
              "win": win, "wout": wout, "prm": prm, "cst": cst, "bout": np.ascontiguousarray(bout)}
    nc = bacc.Bacc("TRN2", target_bir_lowering=False, num_devices=1)
    args = [nc.dram_tensor(f"in_{n}", v.shape, F32, kind="ExternalInput").ap() for n, v in arrays.items()]
    out = nc.dram_tensor("out_0", (TOKENS, D), F32, kind="ExternalOutput").ap()
    macaron(nc, *args, out)
    r = run_bass_kernel_spmd(nc, [{f"in_{n}": v for n, v in arrays.items()}], core_ids=[0])
    return r.results[0]["out_0"].reshape(BATCH, SEQ, D)
```
